# Optimizing a Trainium2 kernel written in Bass

```python
import numpy as np
import jax
import jax.numpy as jnp

def _softmax(x, axis=-1):
    return jax.nn.softmax(x, axis=axis)

def _gelu(x):
    return jax.nn.gelu(x, approximate=True)

def _silu(x):
    return jax.nn.silu(x)

def _sigmoid(x):
    return jax.nn.sigmoid(x)

def _layernorm(x, axis=-1, eps=1e-05):
    m = jnp.mean(x, axis=axis, keepdims=True)
    v = jnp.var(x, axis=axis, keepdims=True)
    return (x - m) / jnp.sqrt(v + eps)

def _scatter_add(tgt, idx, src, axis=0):
    return tgt.at[idx].add(src)

def _segment_sum(src, seg, n):
    return jax.ops.segment_sum(src, seg, n)
kernel_name = 'mk_gps_d1_gnn_r16_032e58'

def setup_inputs(seed: int=0):
    np.random.seed(seed)
    _w = jnp.asarray

    def _rec_inputs():
        import jax
        import jax.numpy as jnp
        _gk = jax.random.key(seed)
        x = -0.0003713 + 1 * jax.random.normal(jax.random.fold_in(_gk, 1), (3125, 256), jnp.float32)
        _s = jax.random.randint(jax.random.fold_in(_gk, 2), (50000,), 0, 3125, jnp.int32)
        _d = jax.random.randint(jax.random.fold_in(_gk, 3), (50000,), 0, 3125, jnp.int32)
        _loop = jnp.arange(3125, dtype=jnp.int32)
        src = jnp.concatenate([_s, _d, _loop])
        dst = jnp.concatenate([_d, _s, _loop])
        _o = jnp.argsort(dst, stable=True)
        src = src[_o]
        dst = dst[_o]
        edge_type_8 = jax.random.randint(jax.random.fold_in(_gk, 12), (103125,), 0, 8, jnp.int32)
        return (x, src, dst, edge_type_8)
    x, src, dst, edge_type_8 = _rec_inputs()

    def _L0_gnn_setup():
        import jax, jax.numpy as jnp
        import numpy as np
        N_NODES = 3125
        N_EDGES = 18750
        N_REL = 8
        D = 256
        N_LAYERS = 3

        def _rgcn_layer(x, W, root, bias, src, dst, seg):
            agg = jax.ops.segment_sum(x[src], seg, num_segments=N_REL * N_NODES)
            agg = agg.reshape(N_REL, N_NODES, -1)
            return jnp.einsum('rnd,rde->ne', agg, W) + x @ root + bias
        key = jax.random.key(seed)
        k1, k2, k3, k4, k5 = jax.random.split(key, 5)
        x = jax.random.normal(k1, (N_NODES, D), dtype=jnp.float32)
        scale = 1.0 / np.sqrt(D)
        weights = jax.random.normal(k2, (N_LAYERS, N_REL, D, D), dtype=jnp.float32) * scale
        roots = jax.random.normal(k3, (N_LAYERS, D, D), dtype=jnp.float32) * scale
        biases = jnp.zeros((N_LAYERS, D), dtype=jnp.float32)
        edge_index = jax.random.randint(k4, (2, N_EDGES), 0, N_NODES, dtype=jnp.int64)
        edge_type = jax.random.randint(k5, (N_EDGES,), 0, N_REL, dtype=jnp.int64)
        return {'x': x, 'weights': weights, 'roots': roots, 'biases': biases, 'edge_index': edge_index, 'edge_type': edge_type}
    _L0_gnn_all = _L0_gnn_setup()
    _L0_gnn_in = {k: v for k, v in _L0_gnn_all.items() if k in ('weights', 'roots', 'biases')}
    del _L0_gnn_all

    def _L0_mix_setup():
        import jax, jax.numpy as jnp
        import numpy as np
        HEADS = 4
        DIM_HEAD = 32
        key = jax.random.key(seed)
        k1, k2, k3 = jax.random.split(key, 3)
        B, L, D = (16, 512, 256)
        hidden = HEADS * DIM_HEAD
        x = jax.random.normal(k1, (B, L, D), dtype=jnp.float32)
        W_qkv = jax.random.normal(k2, (D, 3 * hidden), dtype=jnp.float32) * D ** (-0.5)
        W_out = jax.random.normal(k3, (hidden, D), dtype=jnp.float32) * hidden ** (-0.5)
        b_out = jnp.zeros((D,), dtype=jnp.float32)
        return {'x': x, 'W_qkv': W_qkv, 'W_out': W_out, 'b_out': b_out}
    _L0_mix_all = _L0_mix_setup()
    _L0_mix_in = {k: v for k, v in _L0_mix_all.items() if k in ('W_qkv', 'W_out', 'b_out')}
    del _L0_mix_all

    def _L0_ffn_setup():
        import jax, jax.numpy as jnp
        import numpy as np
        TOP_K = 2
        LN_EPS = 1e-05
        key = jax.random.key(seed)
        ks = jax.random.split(key, 8)
        B, S, D, E, H = (16, 1024, 256, 8, 1024)
        x = jax.random.normal(ks[0], (B, S, D), dtype=jnp.float32)
        Wr = jax.random.normal(ks[1], (D, E), dtype=jnp.float32) * 0.1
        br = jnp.zeros((E,), dtype=jnp.float32)
        ln_g = jnp.ones((E, D), dtype=jnp.float32)
        ln_b = jnp.zeros((E, D), dtype=jnp.float32)
        W1 = jax.random.normal(ks[2], (E, D, H), dtype=jnp.float32) * (1.0 / np.sqrt(D))
        b1 = jnp.zeros((E, H), dtype=jnp.float32)
        W2 = jax.random.normal(ks[3], (E, H, D), dtype=jnp.float32) * (1.0 / np.sqrt(H))
        b2 = jnp.zeros((E, D), dtype=jnp.float32)
        return {'x': x, 'Wr': Wr, 'br': br, 'ln_g': ln_g, 'ln_b': ln_b, 'W1': W1, 'b1': b1, 'W2': W2, 'b2': b2}
    _L0_ffn_all = _L0_ffn_setup()
    _L0_ffn_in = {k: v for k, v in _L0_ffn_all.items() if k in ('Wr', 'br', 'ln_g', 'ln_b', 'W1', 'b1', 'W2', 'b2')}
    del _L0_ffn_all
    return {'x': x, 'src': src, 'dst': dst, 'edge_type_8': edge_type_8, 'L0_gnn_weights': _L0_gnn_in['weights'], 'L0_gnn_roots': _L0_gnn_in['roots'], 'L0_gnn_biases': _L0_gnn_in['biases'], 'L0_mix_W_qkv': _L0_mix_in['W_qkv'], 'L0_mix_W_out': _L0_mix_in['W_out'], 'L0_mix_b_out': _L0_mix_in['b_out'], 'L0_ffn_Wr': _L0_ffn_in['Wr'], 'L0_ffn_br': _L0_ffn_in['br'], 'L0_ffn_ln_g': _L0_ffn_in['ln_g'], 'L0_ffn_ln_b': _L0_ffn_in['ln_b'], 'L0_ffn_W1': _L0_ffn_in['W1'], 'L0_ffn_b1': _L0_ffn_in['b1'], 'L0_ffn_W2': _L0_ffn_in['W2'], 'L0_ffn_b2': _L0_ffn_in['b2']}

def reference(x, src, dst, edge_type_8, L0_gnn_weights, L0_gnn_roots, L0_gnn_biases, L0_mix_W_qkv, L0_mix_W_out, L0_mix_b_out, L0_ffn_Wr, L0_ffn_br, L0_ffn_ln_g, L0_ffn_ln_b, L0_ffn_W1, L0_ffn_b1, L0_ffn_W2, L0_ffn_b2):
    import jax
    import jax.numpy as jnp

    def _L0_gnn_ref(x, weights, roots, biases, edge_index, edge_type):
        import jax, jax.numpy as jnp
        import numpy as np
        N_NODES = 3125
        N_EDGES = 18750
        N_REL = 8
        D = 256
        N_LAYERS = 3

        def _rgcn_layer(x, W, root, bias, src, dst, seg):
            agg = jax.ops.segment_sum(x[src], seg, num_segments=N_REL * N_NODES)
            agg = agg.reshape(N_REL, N_NODES, -1)
            return jnp.einsum('rnd,rde->ne', agg, W) + x @ root + bias
        src, dst = (edge_index[0], edge_index[1])
        seg = edge_type * N_NODES + dst
        h = x
        for l in range(N_LAYERS - 1):
            h = jax.nn.relu(_rgcn_layer(h, weights[l], roots[l], biases[l], src, dst, seg))
        h = jax.nn.sigmoid(_rgcn_layer(h, weights[-1], roots[-1], biases[-1], src, dst, seg))
        return h

    def _L0_mix_ref(x, W_qkv, W_out, b_out):
        import jax, jax.numpy as jnp
        import numpy as np
        HEADS = 4
        DIM_HEAD = 32
        B, L, D = x.shape
        scale = DIM_HEAD ** (-0.5)
        qkv = jnp.einsum('bld,df->blf', x, W_qkv)
        qkv = qkv.reshape(B, L, 3, HEADS, DIM_HEAD)
        q = jnp.transpose(qkv[:, :, 0], (0, 2, 1, 3)) * scale
        k = jax.nn.softmax(jnp.transpose(qkv[:, :, 1], (0, 2, 1, 3)), axis=2)
        v = jnp.transpose(qkv[:, :, 2], (0, 2, 1, 3))
        context = jnp.einsum('bhld,bhle->bhde', k, v)
        out = jnp.einsum('bhde,bhld->bhle', context, q)
        out = jnp.transpose(out, (0, 2, 1, 3)).reshape(B, L, HEADS * DIM_HEAD)
        return jnp.einsum('blf,fd->bld', out, W_out) + b_out

    def _L0_ffn_ref(x, Wr, br, ln_g, ln_b, W1, b1, W2, b2):
        import jax, jax.numpy as jnp
        import numpy as np
        TOP_K = 2
        LN_EPS = 1e-05
        B, S, D = x.shape
        N = B * S
        xt = x.reshape(N, D)
        logits = xt @ Wr + br
        probs = jax.nn.softmax(logits, axis=-1)
        top_p, top_idx = jax.lax.top_k(probs, TOP_K)
        weights = top_p / top_p.sum(axis=-1, keepdims=True)
        mu = xt.mean(axis=-1, keepdims=True)
        var = ((xt - mu) ** 2).mean(axis=-1, keepdims=True)
        xn = (xt - mu) * jax.lax.rsqrt(var + LN_EPS)
        xe = xn[None, :, :] * ln_g[:, None, :] + ln_b[:, None, :]
        h = jax.nn.gelu(jnp.einsum('end,edh->enh', xe, W1) + b1[:, None, :], approximate=False)
        y = jnp.einsum('enh,ehd->end', h, W2) + b2[:, None, :]
        y_tok = jnp.transpose(y, (1, 0, 2))
        sel = jnp.take_along_axis(y_tok, top_idx[:, :, None], axis=1)
        out = (weights[:, :, None] * sel).sum(axis=1)
        return out.reshape(B, S, D)
    edge_index = jnp.stack([src, dst])
    xn = _layernorm(x, axis=-1)
    x = x + _L0_gnn_ref(xn, L0_gnn_weights, L0_gnn_roots, L0_gnn_biases, edge_index, edge_type_8) + _L0_mix_ref(xn[None], L0_mix_W_qkv, L0_mix_W_out, L0_mix_b_out)[0]
    x = x + _L0_ffn_ref(_layernorm(x, axis=-1)[None], L0_ffn_Wr, L0_ffn_br, L0_ffn_ln_g, L0_ffn_ln_b, L0_ffn_W1, L0_ffn_b1, L0_ffn_W2, L0_ffn_b2)[0]
    return x

_drawn_inputs = setup_inputs


def setup_inputs(seed=0):
    import zlib

    import numpy as np

    out = dict(_drawn_inputs(seed))
    spreads = {'L0_gnn_biases': (0.0, 0.1),
     'L0_mix_b_out': (0.0, 0.1),
     'L0_ffn_br': (0.0, 0.1),
     'L0_ffn_ln_g': (1.0, 0.2),
     'L0_ffn_ln_b': (0.0, 0.1),
     'L0_ffn_b1': (0.0, 0.1),
     'L0_ffn_b2': (0.0, 0.1)}
    factors = {}
    for name, (base, spread) in spreads.items():
        noise = np.random.default_rng([zlib.crc32(name.encode()), seed]).standard_normal(out[name].shape)
        drawn = base * np.exp(spread * noise) if base else spread * noise
        out[name] = jnp.asarray(drawn.astype(out[name].dtype))
    for name, factor in factors.items():
        out[name] = (out[name] * factor).astype(out[name].dtype)
    return out
```

```python
import concourse.bass as bass
from concourse import mybir
from contextlib import ExitStack

F32 = mybir.dt.float32
I32 = mybir.dt.int32
U32 = mybir.dt.uint32
ALU = mybir.AluOpType
ACT = mybir.ActivationFunctionType
AXX = mybir.AxisListType.X

P = 128
N_NODES, D = 3125, 256
KD = D // P
NT = -(-N_NODES // P)
NP = NT * P
LAST = N_NODES - (NT - 1) * P
TG = 5
NG = NT // TG
REL, LAYERS = 8, 3
EDGES = 103125
WIN = 64
GWIN = 400
NGW = NP // GWIN
HALF = 5
STEP = 2 * HALF
REAL_TILES = -(-EDGES // P)
STEPS = -(-REAL_TILES // STEP)
ETILES = STEPS * STEP
EC = -(-ETILES // P)
FULL_C = EDGES // (P * P)
FULL_R = (EDGES - FULL_C * P * P) // P
REST = EDGES - FULL_C * P * P - FULL_R * P
NO_NODE = 8192.0
HEADS, DH = 4, 32
HID = HEADS * DH
NCH = 8
EXP, HF = 8, 1024
HC = HF // P
TOK = TG * P
HTOK = TOK // 2
EPS = 1e-5
ARENA = 37500
FFW = 3 * EXP + 3


def gps_layer(nc, x, src, dst, etype, gw, groots, gbias, wqkv, wout, bout,
              Wr, br, ln_g, ln_b, W1, b1, W2, b2, out):
    ctx = ExitStack()
    with ctx:
        ctx.enter_context(nc.allow_non_contiguous_dma(reason="short bias and window columns"))

        def sb(name, shape, dt=F32):
            return ctx.enter_context(nc.sbuf_tensor(name, shape, dt))

        y_dram = [nc.dram_tensor(f"y_dram{i}", (NP * REL, D), F32).ap() for i in range(2)]
        win_dram = nc.dram_tensor("win_dram", (EC * P,), I32).ap()

        xtok = sb("xtok", [P, NT, D])
        hT_all = sb("hT_all", [P, KD, NP])
        ident = sb("ident", [P, P])
        ones = sb("ones", [P, P])
        zcol = sb("zcol", [P, 1])
        iota_w = sb("iota_w", [P, GWIN])
        stats = sb("stats", [P, NT, 6])
        mv = sb("mv", [P, NT, 2])
        rstd = sb("rstd", [P, NT])
        mv2 = sb("mv2", [P, NT, 2])
        rstd2 = sb("rstd2", [P, NT])
        flag = sb("flag", [P, 1], I32)
        arena = sb("arena", [P, ARENA])
        used = [0]

        def carve(n):
            a = arena[:, used[0]:used[0] + n]
            used[0] += n
            assert used[0] <= ARENA, used[0]
            return a

        idx_i = carve(EC * P).bitcast(I32)
        dloc = carve(EC * P)
        dabs = carve(EC * P)
        win_row = carve(EC * P).bitcast(I32)
        bias_g = carve(LAYERS * KD).rearrange("p (l k) -> p l k", l=LAYERS)
        wrel = carve(KD * REL * D).rearrange("p (k n) -> p k n", k=KD)
        wroot = carve(KD * D).rearrange("p (k n) -> p k n", k=KD)
        ybuf = carve(4 * 512).rearrange("p (c n) -> p c n", c=4)
        stage = carve(TG * KD * P).rearrange("p (c k n) -> p c k n", c=TG, k=KD)
        gath = carve(STEP * D).rearrange("p (c n) -> p c n", c=STEP)
        onehot = carve(STEP * WIN).rearrange("p (c n) -> p c n", c=STEP)
        ghot = carve(GWIN)
        gcol = carve(2)
        idx_ring = carve(STEP).bitcast(I32)
        xnt = carve(TG * D).rearrange("p (c n) -> p c n", c=TG)
        wqkv_sb = carve(KD * 3 * HID).rearrange("p (k n) -> p k n", k=KD)
        wout_sb = carve(D)
        bout_sb = carve(D)
        mark = used[0]
        e_src = carve(EC * P).bitcast(I32).rearrange("p (c n) -> p c n", c=EC)
        e_dst = carve(EC * P).bitcast(I32).rearrange("p (c n) -> p c n", c=EC)
        e_typ = carve(EC * P).bitcast(I32).rearrange("p (c n) -> p c n", c=EC)
        e_dstf = carve(EC * P).rearrange("p (c n) -> p c n", c=EC)
        e_idx = carve(EC * P).rearrange("p (c n) -> p c n", c=EC)
        e_loc = carve(EC * P).rearrange("p (c n) -> p c n", c=EC)
        e_in = carve(EC * P).rearrange("p (c n) -> p c n", c=EC)
        e_win = carve(EC)
        e_wini = carve(EC).bitcast(I32)
        e_viol = carve(1)
        used[0] = mark
        qT = carve(NP)
        kT = carve(NP)
        vtok = carve(NP).rearrange("p (t n) -> p t n", t=NT)
        ktok = carve(2 * P).rearrange("p (c n) -> p c n", c=2)
        nkmax = carve(1)
        ksum = carve(1)
        krec = carve(1)
        ctxT = carve(P)
        mctx = carve(D)
        used[0] = 0
        w1s = [carve(KD * HF).rearrange("p (k n) -> p k n", k=KD) for _ in range(2)]
        w2s = [carve(HC * D).rearrange("p (k n) -> p k n", k=HC) for _ in range(2)]
        hid = [carve(HC * HTOK).rearrange("p (k n) -> p k n", k=HC) for _ in range(2)]
        gcols = carve(EXP * KD).rearrange("p (e k) -> p e k", e=EXP)
        bcols = carve(EXP * KD).rearrange("p (e k) -> p e k", e=EXP)
        b1cols = carve(EXP * HC).rearrange("p (e k) -> p e k", e=EXP)
        b1fold = carve(2 * HC).rearrange("p (s k) -> p s k", s=2)
        wr_sb = carve(KD * EXP).rearrange("p (k n) -> p k n", k=KD)
        br_sb = carve(EXP)
        b2_sb = carve(D)
        lg = carve(NT * EXP).rearrange("p (t e) -> p t e", t=NT)
        pr = carve(NT * EXP).rearrange("p (t e) -> p t e", t=NT)
        gate = carve(NT * EXP).rearrange("p (t e) -> p t e", t=NT)
        hit = carve(NT * EXP).rearrange("p (t e) -> p t e", t=NT)
        top = carve(NT * 8).rearrange("p (t e) -> p t e", t=NT)
        topi = carve(NT * 8).bitcast(U32).rearrange("p (t e) -> p t e", t=NT)
        topf = carve(NT * 8).rearrange("p (t e) -> p t e", t=NT)
        rmax = carve(NT)
        rsum = carve(NT)
        rrec = carve(NT)
        gateT = carve(2 * P).rearrange("p (c n) -> p c n", c=2)
        ytok = carve(TG * D).rearrange("p (c n) -> p c n", c=TG)
        yT = carve(TG * KD * P).rearrange("p (c k n) -> p c k n", c=TG, k=KD)

        bank = [ctx.enter_context(nc.psum_tensor(f"bank{i}", [P, 512], F32)) for i in range(8)]

        names = """x_in edge_in gb_in wrel_in mixw_in ffw_in win_out win_in out_st
            const pads edges_made edge_turned edge_back viol_sum flag_set
            var_made sd_made rstd_made xn_made xn_turned stage_full
            y_mm y_act y_dve node_mm root_out qkv_out
            ix_ready tile_mm hot_ready tile_add gen_hot gen_mm gen_add layer_done
            kmax_made kexp_made k_turned k_out ctx_mm ctx_out mctx_mm mctx_out mix_mm mix_add
            sg_made sg_turned sg_add y_made y_stats y_turned y_out xn2_made xn2_turned xn2_out
            router_mm router_in router_exp gates_made gate_turned gate_out b2_mm b2_add
            fold_w fold_mm fold_b hid_mm hid_act out_mm out_acc chain_v chain_p""".split()
        S = {n: ctx.enter_context(nc.semaphore(n)) for n in names}
        s_gath = [ctx.enter_context(nc.semaphore(f"gath{j}")) for j in range(STEP)]
        s_yst = [ctx.enter_context(nc.semaphore(f"y_stored{c}")) for c in range(4)]
        s_w = [ctx.enter_context(nc.semaphore(f"expert_in{c}")) for c in range(2)]
        block = ctx.enter_context(nc.Block())

        def wait(eng, s, v):
            if isinstance(v, int) and v <= 0:
                return
            eng.wait_ge(S[s] if isinstance(s, str) else s, v)

        def wait_apart(eng, s, v):
            wait(eng, s, v)
            eng.nop(nofuse=True)

        def steps(eng, n, body):
            body(0)
            with eng.Fori(1, n) as i:
                body(i)

        def tile_of(a, t):
            return a[:, bass.ds(t, 1), :].rearrange("p o n -> p (o n)")

        w_rel = gw.rearrange("l r (k p) n -> l p k r n", p=P)
        w_root = groots.rearrange("l (k p) n -> l p k n", p=P)

        @block.sync
        def _(sp):
            sp.dma_start(xtok[:, 0:NT - 1, :], x[0:(NT - 1) * P, :].rearrange("(t p) d -> p t d", p=P)).then_inc(S["x_in"], 16)
            sp.wait_ge(S["pads"], 1)
            sp.dma_start(xtok[0:LAST, NT - 1, :], x[(NT - 1) * P:N_NODES, :]).then_inc(S["x_in"], 16)

            def layer_weights(l):
                for k in range(KD):
                    sp.dma_start(wrel[:, k, :].rearrange("p (r n) -> p r n", r=REL), w_rel[l][:, k]).then_inc(S["wrel_in"], 16)
                sp.dma_start(wroot, w_root[l]).then_inc(S["wrel_in"], 16)

            layer_weights(0)
            sp.wait_ge(S["pads"], 4)
            at0, at1 = FULL_C * P * P, FULL_C * P * P + FULL_R * P
            for a, e in ((src, e_src), (dst, e_dst), (etype, e_typ)):
                sp.dma_start(e[:, 0:FULL_C, :], a[0:at0].rearrange("(c p l) -> p c l", p=P, l=P)).then_inc(S["edge_in"], 16)
                sp.dma_start(e[0:FULL_R, FULL_C, :], a[at0:at1].rearrange("(p l) -> p l", l=P)).then_inc(S["edge_in"], 16)
                sp.dma_start(e[FULL_R:FULL_R + 1, FULL_C, 0:REST], a[at1:EDGES].rearrange("(p l) -> p l", p=1)).then_inc(S["edge_in"], 16)
            sp.dma_start(wqkv_sb, wqkv.rearrange("(k p) n -> p k n", p=P)).then_inc(S["mixw_in"], 16)
            sp.dma_start(wout_sb, wout).then_inc(S["mixw_in"], 16)
            sp.dma_start(bout_sb[0:1, :], bout.rearrange("(o n) -> o n", o=1)).then_inc(S["mixw_in"], 16)
            for l in range(LAYERS):
                sp.dma_start(bias_g[:, l, :], gbias[l].rearrange("(k p) -> p k", p=P)).then_inc(S["gb_in"], 16)
            sp.wait_ge(S["edges_made"], 1)
            sp.dma_start(win_dram.rearrange("(c p) -> p c", p=P), e_wini).then_inc(S["win_out"], 16)
            sp.wait_ge(S["win_out"], 16)
            sp.dma_start(win_row[0:1, :], win_dram.rearrange("(o n) -> o n", o=1)).then_inc(S["win_in"], 16)

            for l in range(LAYERS):
                yd = y_dram[l % 2].rearrange("(t p r) d -> p t (r d)", p=P, r=REL)

                def store(t):
                    for c in range(4):
                        wait(sp, "y_act" if c % 2 == 0 else "y_dve", 2 * NT * l + 2 * t + c // 2 + 1)
                        sp.dma_start(yd[:, bass.ds(t, 1), c * 512:(c + 1) * 512].rearrange("p o n -> p (o n)"),
                                     ybuf[:, c, :]).then_inc(s_yst[c], 16)

                steps(sp, NT, store)
                if l + 1 < LAYERS:
                    sp.wait_ge(S["node_mm"], NT * (l + 1))
                    layer_weights(l + 1)
            for c in range(4):
                sp.wait_ge(s_yst[c], 16 * NT * LAYERS)

            sp.wait_ge(S["layer_done"], LAYERS)
            for a, b in ((gcols, ln_g.rearrange("e (k p) -> p e k", p=P)), (bcols, ln_b.rearrange("e (k p) -> p e k", p=P)),
                         (b1cols, b1.rearrange("e (k p) -> p e k", p=P))):
                for e in range(EXP):
                    sp.dma_start(a[:, e, :], b[:, e, :]).then_inc(S["ffw_in"], 16)
            sp.dma_start(wr_sb, Wr.rearrange("(k p) n -> p k n", p=P)).then_inc(S["ffw_in"], 16)
            sp.dma_start(br_sb[0:1, :], br.rearrange("(o n) -> o n", o=1)).then_inc(S["ffw_in"], 16)
            sp.dma_start(b2_sb[0:EXP, :], b2).then_inc(S["ffw_in"], 16)
            for e in range(EXP):
                if e >= 2:
                    sp.wait_ge(S["out_acc"], NT * (e - 1))
                sp.dma_start(w1s[e % 2], W1[e].rearrange("(k p) n -> p k n", p=P)).then_inc(s_w[e % 2], 16)
                sp.dma_start(w2s[e % 2], W2[e].rearrange("(k p) n -> p k n", p=P)).then_inc(s_w[e % 2], 16)
            sp.wait_ge(S["out_acc"], NT * EXP)
            sp.dma_start(out[0:(NT - 1) * P, :].rearrange("(t p) d -> p t d", p=P), xtok[:, 0:NT - 1, :]).then_inc(S["out_st"], 16)
            sp.dma_start(out[(NT - 1) * P:N_NODES, :], xtok[0:LAST, NT - 1, :]).then_inc(S["out_st"], 16)
            sp.wait_ge(S["out_st"], 32)

        @block.gpsimd
        def _(pool):
            nc.gpsimd.memset(xtok[:, NT - 1, :], 0.0).then_inc(S["pads"], 1)
            nc.gpsimd.memset(e_src, 0).then_inc(S["pads"], 1)
            nc.gpsimd.memset(e_typ, 0).then_inc(S["pads"], 1)
            nc.gpsimd.memset(e_dst, int(NO_NODE)).then_inc(S["pads"], 1)
            nc.gpsimd.memset(ones[:, :], 1.0).then_inc(S["const"], 1)
            nc.gpsimd.iota(iota_w[:, :], [[1, GWIN]], base=0, channel_multiplier=0,
                           allow_small_or_imprecise_dtypes=True).then_inc(S["const"], 1)
            nc.gpsimd.memset(ident[:, :], 0.0).then_inc(S["const"], 1)
            pool.wait_ge(S["const"], 3)
            nc.gpsimd.affine_select(out=ident[:, :], in_=ident[:, :], compare_op=ALU.not_equal, fill=1.0, base=0,
                                    pattern=[[-1, P]], channel_multiplier=1).then_inc(S["const"], 1)
            for l in range(LAYERS):
                for c in range(4):
                    pool.wait_ge(s_yst[c], 16 * NT * (l + 1))
                yd = y_dram[l % 2]

                def gather(i):
                    for h in range(2):
                        wait(pool, "ix_ready", 2 * STEPS * l + 2 * i + h + 1)
                        pool.nop(nofuse=True)
                        for j in range(h * HALF, h * HALF + HALF):
                            nc.gpsimd.indirect_dma_start(
                                out=gath[:, j, :], out_offset=None, in_=yd,
                                in_offset=bass.IndirectOffsetOnAxis(ap=idx_ring[:, j:j + 1], axis=0)).then_inc(s_gath[j], 16)

                steps(pool, STEPS, gather)

        @block.scalar
        def _(act):
            act.wait_ge(S["var_made"], 1)
            nc.scalar.activation(rstd[:, :], mv[:, :, 1], ACT.Sqrt).then_inc(S["sd_made"], 1)
            for b, (o, n0, n1) in enumerate(((idx_i, 0, 4), (idx_i, 4, EC), (dloc, 0, 4), (dloc, 4, EC), (dabs, 0, 4), (dabs, 4, EC))):
                act.wait_ge(S["edge_turned"], b + 1)
                nc.scalar.copy(o[:, n0 * P:n1 * P], bank[b][:, 0:(n1 - n0) * P]).then_inc(S["edge_back"], 1)
            act.wait_ge(S["gb_in"], 16 * LAYERS)
            for l in range(LAYERS):
                if l > 0:
                    act.wait_ge(S["layer_done"], l)

                def node_out(i):
                    if l > 0:
                        for j in range(TG):
                            t = TG * i + j
                            wait_apart(act, "node_mm", NT * l + t + 1 - TG)
                            nc.scalar.activation(stage[:, j, :, :], hT_all[:, :, bass.ds(TOK * i + P * j, P)],
                                                 ACT.Relu).then_inc(S["stage_full"], 1)
                    else:
                        for j in range(TG):
                            t = TG * i + j
                            wait(act, "xn_turned", t + 1)
                            wait(act, "node_mm", t + 1 - TG)
                            nc.scalar.copy(stage[:, j, :, :], bank[6 + j % 2][:, 0:D].rearrange("p (k n) -> p k n", k=KD)).then_inc(S["stage_full"], 1)
                    for j in range(TG):
                        t = TG * i + j
                        for c in (0, 2):
                            wait(act, "y_mm", 4 * NT * l + 4 * t + c + 1)
                            wait(act, s_yst[c], 16 * (NT * l + t))
                            nc.scalar.copy(ybuf[:, c, :], bank[c][:, :]).then_inc(S["y_act"], 1)
                        wait_apart(act, "node_mm", NT * l + t + 1)
                        for e in range(KD):
                            nc.scalar.activation(hT_all[:, e, bass.ds(TOK * i + P * j, P)], bank[4][:, e * P:(e + 1) * P],
                                                 ACT.Identity, bias=bias_g[:, l, e:e + 1]).then_inc(S["root_out"], 1)

                steps(act, NG, node_out)
                if l == 0:
                    act.wait_ge(S["kmax_made"], 1)
                    nc.scalar.activation(kT[:, 0:N_NODES], kT[:, 0:N_NODES], ACT.Exp, bias=nkmax, accum_out=ksum).then_inc(S["kexp_made"], 1)

                def ring(i):
                    for h in range(2):
                        wait(act, "tile_mm", ETILES * l + STEP * i + HALF * (h - 1))
                        nc.scalar.copy(idx_ring[:, h * HALF:(h + 1) * HALF],
                                       idx_i[:, bass.ds(STEP * i + h * HALF, HALF)]).then_inc(S["ix_ready"], 1)

                steps(act, STEPS, ring)
            act.wait_ge(S["layer_done"], LAYERS)

            def sigmoid(i):
                for j in range(TG):
                    wait_apart(act, "sg_turned", TG * i + j + 1 - TG)
                    nc.scalar.activation(yT[:, j, :, :], hT_all[:, :, bass.ds(TOK * i + P * j, P)], ACT.Sigmoid).then_inc(S["sg_made"], 1)

            steps(act, NG, sigmoid)
            act.wait_ge(S["var_made"], 2)
            nc.scalar.activation(rstd[:, :], mv[:, :, 1], ACT.Sqrt).then_inc(S["sd_made"], 1)
            act.wait_ge(S["sg_turned"], NT)

            def y_back(i):
                for j in range(TG):
                    t = TG * i + j
                    wait(act, "y_turned", t + 1)
                    wait(act, "router_mm", t + 1 - TG)
                    nc.scalar.copy(yT[:, j, :, :], bank[j % 2][:, 0:D].rearrange("p (k n) -> p k n", k=KD)).then_inc(S["y_out"], 1)

            steps(act, NG, y_back)
            act.wait_ge(S["var_made"], 3)
            nc.scalar.activation(rstd2[:, :], mv2[:, :, 1], ACT.Sqrt).then_inc(S["sd_made"], 1)

            def xn2_back(i):
                for j in range(TG):
                    wait(act, "xn2_turned", TG * i + j + 1)
                    nc.scalar.copy(hT_all[:, :, bass.ds(TOK * i + P * j, P)],
                                   bank[j % 2][:, 0:D].rearrange("p (k n) -> p k n", k=KD)).then_inc(S["xn2_out"], 1)

            steps(act, NG, xn2_back)
            act.wait_ge(S["router_in"], 1)
            nc.scalar.activation(pr, lg, ACT.Exp).then_inc(S["router_exp"], 1)
            for e in range(EXP):
                act.wait_ge(S["fold_b"], e + 1)
                base = e * NG * 2 * HC

                def gelu(i):
                    for h in range(2):
                        wait(act, "out_mm", NT * e + TG * i - TG + (3 if h == 0 else TG))
                        for q in range(HC):
                            wait(act, "hid_mm", base + i * 2 * HC + h * HC + q + 1)
                            nc.scalar.activation(hid[h][:, q, :], bank[q % 3][:, 0:HTOK], ACT.Gelu,
                                                 bias=b1fold[:, e % 2, q:q + 1]).then_inc(S["hid_act"], 1)

                steps(act, NG, gelu)

        @block.vector
        def _(dve):
            chain = [0]

            def link(ins):
                chain[0] += 1
                ins.then_inc(S["chain_v"], 1)
                dve.wait_ge(S["chain_v"], chain[0])

            def fence():
                link(nc.vector.memset(zcol[:, :], 0.0))

            def row_stats(rows):
                with dve.Fori(0, NT) as t:
                    nc.vector.bn_stats(tile_of(stats, t), tile_of(rows, t))
                fence()
                for t in range(NT):
                    nc.vector.bn_aggr(mv[:, t, :], stats[:, t, :])
                fence()
                nc.vector.tensor_scalar(mv[:, :, 1], mv[:, :, 1], EPS, None, ALU.add).then_inc(S["var_made"], 1)

            dve.wait_ge(S["const"], 4)
            dve.wait_ge(S["x_in"], 32)
            row_stats(xtok)
            dve.wait_ge(S["edge_in"], 9 * 16)
            link(nc.vector.tensor_copy(e_dstf, e_dst))
            nc.vector.scalar_tensor_tensor(out=e_idx, in0=e_src, scalar=float(REL), in1=e_typ, op0=ALU.mult, op1=ALU.add)
            link(nc.vector.tensor_reduce(out=e_win, in_=e_dstf, op=ALU.min, axis=AXX))
            link(nc.vector.tensor_scalar(e_win, e_win, float(NP - WIN), None, ALU.min))
            nc.vector.tensor_copy(e_wini, e_win).then_inc(S["edges_made"], 1)
            link(nc.vector.tensor_tensor(e_loc, e_dstf, e_win.unsqueeze(2).to_broadcast([P, EC, P]), ALU.subtract))
            nc.vector.memset(zcol[:, :], 0.0).then_inc(S["edges_made"], 1)
            link(nc.vector.tensor_scalar(e_in, e_dstf, NO_NODE / 2, None, ALU.is_lt))
            link(nc.vector.scalar_tensor_tensor(out=e_in, in0=e_loc, scalar=float(WIN), in1=e_in, op0=ALU.is_ge, op1=ALU.mult))
            nc.vector.tensor_reduce(out=e_viol, in_=e_in.rearrange("p c n -> p (c n)"), op=ALU.add, axis=AXX).then_inc(S["edges_made"], 1)
            dve.wait_ge(S["viol_sum"], 1)
            nc.vector.tensor_scalar(flag[:, :], bank[6][:, 0:1], 1.0, None, ALU.min).then_inc(S["flag_set"], 1)
            dve.wait_ge(S["sd_made"], 1)
            link(nc.vector.reciprocal(rstd[:, :], rstd[:, :]))

            for l in range(LAYERS):
                def node_out(i):
                    if l == 0:
                        for j in range(TG):
                            t = TG * i + j
                            wait(dve, "xn_turned", t + 1 - TG)
                            nc.vector.tensor_scalar(xnt[:, j, :], tile_of(xtok, t), mv[:, bass.ds(t, 1), 0],
                                                    rstd[:, bass.ds(t, 1)], ALU.subtract, ALU.mult).then_inc(S["xn_made"], 1)
                    for j in range(TG):
                        t = TG * i + j
                        for c in (1, 3):
                            wait(dve, "y_mm", 4 * NT * l + 4 * t + c + 1)
                            wait(dve, s_yst[c], 16 * (NT * l + t))
                            nc.vector.tensor_copy(ybuf[:, c, :], bank[c][:, :]).then_inc(S["y_dve"], 1)
                        if l == 0:
                            wait(dve, "node_mm", t + 1)
                            nc.vector.tensor_copy(qT[:, bass.ds(TOK * i + P * j, P)], bank[5][:, 0:P])
                            nc.vector.tensor_copy(kT[:, bass.ds(TOK * i + P * j, P)], bank[5][:, P:2 * P])
                            nc.vector.tensor_copy(tile_of(vtok, t), bank[5][:, 2 * P:3 * P]).then_inc(S["qkv_out"], 1)

                steps(dve, NG, node_out)
                if l == 0:
                    fence()
                    link(nc.vector.reduce_max(nkmax, kT[:, 0:N_NODES], AXX))
                    nc.vector.tensor_scalar(nkmax, nkmax, -1.0, None, ALU.mult).then_inc(S["kmax_made"], 1)
                    for t in range(NT):
                        dve.wait_ge(S["k_turned"], t + 1)
                        nc.vector.tensor_copy(ktok[:, t % 2, :], bank[t % 2][:, 0:P]).then_inc(S["k_out"], 1)
                    link(nc.vector.reciprocal(krec, ksum))
                    link(nc.vector.tensor_scalar(krec, krec, float(DH) ** -0.5, None, ALU.mult))
                    link(nc.vector.memset(ctxT, 0.0))
                    dve.wait_ge(S["ctx_mm"], NT)
                    for h in range(HEADS):
                        r = slice(h * DH, (h + 1) * DH)
                        last = nc.vector.tensor_copy(ctxT[r, r], bank[2][r, r])
                    last.then_inc(S["ctx_out"], 1)
                    dve.wait_ge(S["mctx_mm"], 1)
                    nc.vector.tensor_scalar(mctx, bank[3][:, 0:D], krec, None, ALU.mult).then_inc(S["mctx_out"], 1)
                    for t in range(NT):
                        dve.wait_ge(S["mix_mm"], t + 1)
                        nc.vector.tensor_tensor(xtok[:, t, :], xtok[:, t, :], bank[4 + t % 4][:, 0:D], ALU.add).then_inc(S["mix_add"], 1)
                    dve.wait_ge(S["win_in"], 16)
                    dve.wait_ge(S["edge_back"], 6)
                dve.wait_ge(S["root_out"], KD * NT * (l + 1))
                outside = dve.value_load(flag[0:1, 0:1], min_val=0, max_val=1)
                with dve.If(outside < 1):
                    def hot(i, h):
                        nc.vector.tensor_tensor(
                            onehot[:, h * HALF:(h + 1) * HALF, :],
                            iota_w[:, 0:WIN].unsqueeze(1).to_broadcast([P, HALF, WIN]),
                            dloc[:, bass.ds(STEP * i + h * HALF, HALF)].unsqueeze(2).to_broadcast([P, HALF, WIN]),
                            ALU.is_equal).then_inc(S["hot_ready"], 1)

                    hot(0, 0)
                    hot(0, 1)

                    def adds(i):
                        _, wins = nc.values_load_multi_w_load_instructions(
                            win_row[0:1, bass.ds(STEP * i, STEP)], engines=(dve.engine,), min_val=0, max_val=NP - WIN,
                            skip_runtime_bounds_check_because="clamped when they were made")
                        for h in range(2):
                            for j in range(h * HALF, h * HALF + HALF):
                                n = ETILES * l + STEP * i + j
                                wait(dve, "tile_mm", n + 1)
                                wait(dve, "tile_add", n)
                                a = hT_all[:, :, bass.ds(wins[j], WIN)]
                                nc.vector.tensor_tensor(a, a, bank[j % 2][:, 0:KD * WIN].rearrange("p (k n) -> p k n", k=KD),
                                                        ALU.add).then_inc(S["tile_add"], 1)
                            hot(i + 1, h)

                    steps(dve, STEPS, adds)
                    dve.wait_ge(S["tile_add"], ETILES * (l + 1))
                with dve.Else():
                    with dve.Fori(0, ETILES) as n:
                        nc.vector.tensor_copy(gcol[:, 0:1], dabs[:, bass.ds(n, 1)]).then_inc(S["gen_hot"], 1)
                        with dve.Fori(0, NGW) as v:
                            g = (n + ETILES * l) * NGW + v
                            dve.wait_ge(S["gen_hot"], (n + ETILES * l) * (2 * NGW + 1) + v * 2 + 1)
                            nc.vector.tensor_scalar(ghot, iota_w[:, :], gcol[:, 0:1], None, ALU.is_equal).then_inc(S["gen_hot"], 1)
                            dve.wait_ge(S["gen_hot"], (n + ETILES * l) * (2 * NGW + 1) + v * 2 + 2)
                            nc.vector.tensor_scalar(gcol[:, 0:1], gcol[:, 0:1], float(-GWIN), None, ALU.add).then_inc(S["gen_hot"], 1)
                            dve.wait_ge(S["gen_mm"], g + 1)
                            for k in range(KD):
                                a = hT_all[:, k, bass.ds(v * GWIN, GWIN)]
                                nc.vector.tensor_tensor(a, a, bank[k][:, 0:GWIN], ALU.add).then_inc(S["gen_add"], 1)
                            dve.wait_ge(S["gen_add"], (g + 1) * KD)
                nc.vector.memset(zcol[:, :], 0.0).then_inc(S["layer_done"], 1)

            def gnn_add(i):
                for j in range(TG):
                    t = TG * i + j
                    wait(dve, "sg_turned", t + 1)
                    nc.vector.tensor_tensor(tile_of(xtok, t), tile_of(xtok, t), bank[j % 2][:, 0:D], ALU.add).then_inc(S["sg_add"], 1)

            steps(dve, NG, gnn_add)
            dve.wait_ge(S["sg_add"], NT)
            row_stats(xtok)
            dve.wait_ge(S["sd_made"], 2)
            link(nc.vector.reciprocal(rstd[:, :], rstd[:, :]))

            def normed(i, j, s, slot_free):
                t = TG * i + j
                wait(dve, s, slot_free)
                return nc.vector.tensor_scalar(ytok[:, j, :], tile_of(xtok, t), mv[:, bass.ds(t, 1), 0],
                                               rstd[:, bass.ds(t, 1)], ALU.subtract, ALU.mult)

            def y_rows(i):
                for j in range(TG):
                    wait(dve, "y_stats", TG * i + j + 1 - TG)
                    normed(i, j, "y_turned", TG * i + j + 1 - TG).then_inc(S["y_made"], 1)
                for j in range(TG):
                    t = TG * i + j
                    wait(dve, "y_made", t + 1)
                    nc.vector.bn_stats(tile_of(stats, t), ytok[:, j, :]).then_inc(S["y_stats"], 1)

            steps(dve, NG, y_rows)
            fence()
            for t in range(NT):
                nc.vector.bn_aggr(mv2[:, t, :], stats[:, t, :])
            fence()
            nc.vector.tensor_scalar(mv2[:, :, 1], mv2[:, :, 1], EPS, None, ALU.add).then_inc(S["var_made"], 1)
            dve.wait_ge(S["sd_made"], 3)
            link(nc.vector.reciprocal(rstd2[:, :], rstd2[:, :]))
            dve.wait_ge(S["y_turned"], NT)

            def xn2_rows(i):
                for j in range(TG):
                    normed(i, j, "xn2_turned", TG * i + j + 1 - TG).then_inc(S["y_made"], 1)
                for j in range(TG):
                    t = TG * i + j
                    wait(dve, "y_made", NT + t + 1)
                    nc.vector.tensor_scalar(ytok[:, j, :], ytok[:, j, :], mv2[:, bass.ds(t, 1), 0],
                                            rstd2[:, bass.ds(t, 1)], ALU.subtract, ALU.mult).then_inc(S["xn2_made"], 1)

            steps(dve, NG, xn2_rows)
            bc = lambda a: a.unsqueeze(2).to_broadcast([P, NT, EXP])
            dve.wait_ge(S["router_mm"], NT)
            link(nc.vector.tensor_copy(lg, bank[5][:, 0:NT * EXP].rearrange("p (t e) -> p t e", t=NT)))
            link(nc.vector.tensor_reduce(out=rmax, in_=lg, op=ALU.max, axis=AXX))
            nc.vector.tensor_tensor(lg, lg, bc(rmax), ALU.subtract).then_inc(S["router_in"], 1)
            dve.wait_ge(S["router_exp"], 1)
            link(nc.vector.tensor_reduce(out=rsum, in_=pr, op=ALU.add, axis=AXX))
            link(nc.vector.reciprocal(rrec, rsum))
            link(nc.vector.tensor_tensor(pr, pr, bc(rrec), ALU.mult))
            for t in range(NT):
                last = nc.vector.max(top[:, t, :], pr[:, t, :])
            link(last)
            for t in range(NT):
                last = nc.vector.max_index(topi[:, t, :], top[:, t, :], pr[:, t, :])
            link(last)
            link(nc.vector.tensor_copy(topf, topi))
            link(nc.vector.tensor_tensor(rsum, top[:, :, 0], top[:, :, 1], ALU.add))
            link(nc.vector.reciprocal(rrec, rsum))
            link(nc.vector.tensor_tensor(top[:, :, 0:2], top[:, :, 0:2], rrec.unsqueeze(2).to_broadcast([P, NT, 2]), ALU.mult))
            eid = iota_w[:, 0:EXP].unsqueeze(1).to_broadcast([P, NT, EXP])
            link(nc.vector.tensor_tensor(gate, eid, bc(topf[:, :, 0]), ALU.is_equal))
            link(nc.vector.tensor_tensor(gate, gate, bc(top[:, :, 0]), ALU.mult))
            link(nc.vector.tensor_tensor(hit, eid, bc(topf[:, :, 1]), ALU.is_equal))
            link(nc.vector.tensor_tensor(hit, hit, bc(top[:, :, 1]), ALU.mult))
            nc.vector.tensor_tensor(gate, gate, hit, ALU.add).then_inc(S["gates_made"], 1)
            for t in range(NT):
                dve.wait_ge(S["gate_turned"], t + 1)
                if t >= 2:
                    dve.wait_ge(S["b2_mm"], t - 1)
                nc.vector.tensor_copy(gateT[0:EXP, t % 2, :], bank[t % 2][0:EXP, 0:P]).then_inc(S["gate_out"], 1)
                dve.wait_ge(S["b2_mm"], t + 1)
                nc.vector.tensor_tensor(xtok[:, t, :], xtok[:, t, :], bank[2 + t % 2][:, 0:D], ALU.add).then_inc(S["b2_add"], 1)

            def fold(e):
                dve.wait_ge(s_w[e % 2], 32 * (e // 2 + 1))
                dve.wait_ge(S["fold_mm"], e + 1)
                if e >= 2:
                    dve.wait_ge(S["hid_act"], (e - 1) * NG * 2 * HC)
                for k in range(KD):
                    nc.vector.tensor_scalar(w1s[e % 2][:, k, :], w1s[e % 2][:, k, :], gcols[:, e, k:k + 1], None,
                                            ALU.mult).then_inc(S["fold_w"], 1)
                nc.vector.tensor_tensor(b1fold[:, e % 2, :], b1cols[:, e, :], bank[6][:, 0:HC], ALU.add).then_inc(S["fold_b"], 1)

            dve.wait_ge(S["ffw_in"], 16 * FFW)
            dve.wait_ge(S["b2_add"], NT)
            fold(0)
            for e in range(EXP):
                def accumulate(i):
                    for j in range(TG):
                        t = TG * i + j
                        wait(dve, "out_mm", NT * e + t + 1)
                        if e:
                            wait(dve, "out_acc", NT * (e - 1) + t + 1)
                        nc.vector.scalar_tensor_tensor(out=tile_of(xtok, t), in0=bank[3 + j % 3][:, 0:D],
                                                       scalar=gate[:, bass.ds(t, 1), e], in1=tile_of(xtok, t),
                                                       op0=ALU.mult, op1=ALU.add).then_inc(S["out_acc"], 1)

                accumulate(0)
                if e + 1 < EXP:
                    fold(e + 1)
                with dve.Fori(1, NG) as i:
                    accumulate(i)

        @block.tensor
        def _(pe):
            pe.wait_ge(S["const"], 4)
            pe.wait_ge(S["edges_made"], 2)
            for b, (a, n0, n1) in enumerate(((e_idx, 0, 4), (e_idx, 4, EC), (e_loc, 0, 4), (e_loc, 4, EC), (e_dstf, 0, 4), (e_dstf, 4, EC))):
                for c in range(n0, n1):
                    m = nc.tensor.transpose(bank[b][:, (c - n0) * P:(c - n0 + 1) * P], a[:, c, :], ident[:, :])
                m.then_inc(S["edge_turned"], 1)
            pe.wait_ge(S["edges_made"], 3)
            nc.tensor.matmul(bank[6][:, 0:1], ones[:, :], e_viol, start=True, stop=True).then_inc(S["viol_sum"], 1)
            pe.wait_ge(S["edge_back"], 6)
            pe.wait_ge(S["flag_set"], 1)

            for l in range(LAYERS):
                pe.wait_ge(S["wrel_in"], 48 * (l + 1))
                if l == 0:
                    pe.wait_ge(S["mixw_in"], 48)
                    pe.wait_ge(S["win_out"], 16)

                def node(i):
                    if l == 0:
                        for j in range(TG):
                            t = TG * i + j
                            wait(pe, "xn_made", t + 1)
                            wait(pe, "stage_full", t if j == 0 else t - 1)
                            for k in range(KD):
                                m = nc.tensor.transpose(bank[6 + j % 2][:, k * P:(k + 1) * P], xnt[:, j, k * P:(k + 1) * P], ident[:, :])
                            m.then_inc(S["xn_turned"], 1)
                    for j in range(TG):
                        t = TG * i + j
                        wait(pe, "stage_full", NT * l + t + 1)
                        for c in range(4):
                            wait(pe, "y_act" if c % 2 == 0 else "y_dve", 2 * NT * l + 2 * t + c // 2 - 1)
                            for k in range(KD):
                                m = nc.tensor.matmul(bank[c][:, :], stage[:, j, k, :], wrel[:, k, c * 512:(c + 1) * 512],
                                                     start=k == 0, stop=k == KD - 1)
                            m.then_inc(S["y_mm"], 1)
                        wait(pe, "root_out", KD * (NT * l + t))
                        if l == 0:
                            wait(pe, "qkv_out", t)
                            for o in range(3):
                                for k in range(KD):
                                    w = wqkv_sb[:, k, o * P:(o + 1) * P]
                                    h = stage[:, j, k, :]
                                    nc.tensor.matmul(bank[5][:, o * P:(o + 1) * P], h if o == 2 else w, w if o == 2 else h,
                                                     start=k == 0, stop=k == KD - 1)
                        for e in range(KD):
                            for k in range(KD):
                                m = nc.tensor.matmul(bank[4][:, e * P:(e + 1) * P], wroot[:, k, e * P:(e + 1) * P], stage[:, j, k, :],
                                                     start=k == 0, stop=k == KD - 1)
                        m.then_inc(S["node_mm"], 1)

                steps(pe, NG, node)
                if l == 0:
                    pe.wait_ge(S["kexp_made"], 1)
                    for t in range(NT + 1):
                        if t < NT:
                            rows = P if t < NT - 1 else LAST
                            if t >= 2:
                                pe.wait_ge(S["k_out"], t - 1)
                            nc.tensor.transpose(bank[t % 2][0:rows, 0:P], kT[:, t * P:t * P + rows], ident[:, :]).then_inc(S["k_turned"], 1)
                        if t >= 1:
                            rows = P if t < NT else LAST
                            pe.wait_ge(S["k_out"], t)
                            nc.tensor.matmul(bank[2][:, 0:P], vtok[0:rows, t - 1, :], ktok[0:rows, (t - 1) % 2, :],
                                             start=t == 1, stop=t == NT).then_inc(S["ctx_mm"], 1)
                    pe.wait_ge(S["ctx_out"], 1)
                    nc.tensor.matmul(bank[3][:, 0:D], ctxT, wout_sb, start=True, stop=True).then_inc(S["mctx_mm"], 1)
                    pe.wait_ge(S["mctx_out"], 1)
                    pe.wait_ge(S["root_out"], KD * NT)
                    for t in range(NT):
                        if t >= 4:
                            pe.wait_ge(S["mix_add"], t - 3)
                        nc.tensor.matmul(bank[4 + t % 4][:, 0:D], qT[:, t * P:(t + 1) * P], mctx, start=True, stop=False)
                        nc.tensor.matmul(bank[4 + t % 4][:, 0:D], ones[0:1, :], bout_sb[0:1, :], start=False, stop=True).then_inc(S["mix_mm"], 1)
                pe.wait_ge(S["y_act"], 2 * NT * (l + 1))
                pe.wait_ge(S["y_dve"], 2 * NT * (l + 1))
                outside = pe.value_load(flag[0:1, 0:1], min_val=0, max_val=1)
                with pe.If(outside < 1):
                    def tiles(i):
                        for j in range(STEP):
                            n = ETILES * l + STEP * i + j
                            if j % HALF == 0:
                                wait(pe, "hot_ready", 2 * (STEPS + 1) * l + 2 * i + j // HALF + 1)
                            wait(pe, s_gath[j], 16 * (STEPS * l + i + 1))
                            wait(pe, "tile_add", n - 1)
                            for k in range(KD):
                                m = nc.tensor.matmul(bank[j % 2][:, k * WIN:(k + 1) * WIN], gath[:, j, k * P:(k + 1) * P],
                                                     onehot[:, j, :], start=True, stop=True)
                            m.then_inc(S["tile_mm"], 1)

                    steps(pe, STEPS, tiles)
                with pe.Else():
                    with pe.Fori(0, STEPS) as i:
                        for j in range(STEP):
                            n = ETILES * l + i * STEP + j
                            pe.wait_ge(s_gath[j], (i + (STEPS * l + 1)) * 16)
                            pe.nop(nofuse=True)
                            with pe.Fori(0, NGW) as v:
                                pe.wait_ge(S["gen_hot"], n * (2 * NGW + 1) + v * 2 + 2)
                                for k in range(KD):
                                    m = nc.tensor.matmul(bank[k][:, 0:GWIN], gath[:, j, k * P:(k + 1) * P], ghot,
                                                         start=True, stop=True)
                                m.then_inc(S["gen_mm"], 1)
                            pe.wait_ge(S["gen_add"], (n + 1) * NGW * KD)
                            pe.nop(nofuse=True).then_inc(S["tile_mm"], 1)

            pe.wait_ge(S["layer_done"], LAYERS)

            def gnn_turn(i):
                for j in range(TG):
                    t = TG * i + j
                    wait(pe, "sg_made", t + 1)
                    wait(pe, "sg_add", t if j == 0 else t - 1)
                    for k in range(KD):
                        m = nc.tensor.transpose(bank[j % 2][:, k * P:(k + 1) * P], yT[:, j, k, :], ident[:, :])
                    m.then_inc(S["sg_turned"], 1)

            steps(pe, NG, gnn_turn)
            pe.wait_ge(S["sg_add"], NT)
            pe.wait_ge(S["ffw_in"], 16 * FFW)

            def router(i):
                for j in range(TG):
                    t = TG * i + j
                    wait(pe, "y_made", t + 1)
                    wait(pe, "y_out", t if j == 0 else t - 1)
                    for k in range(KD):
                        m = nc.tensor.transpose(bank[j % 2][:, k * P:(k + 1) * P], ytok[:, j, k * P:(k + 1) * P], ident[:, :])
                    m.then_inc(S["y_turned"], 1)
                for j in range(TG):
                    t = TG * i + j
                    wait(pe, "y_out", t + 1)
                    o = bank[5][:, bass.ds(t * EXP, EXP)]
                    for k in range(KD):
                        nc.tensor.matmul(o, yT[:, j, k, :], wr_sb[:, k, :], start=k == 0, stop=False)
                    nc.tensor.matmul(o, ones[0:1, :], br_sb[0:1, :], start=False, stop=True).then_inc(S["router_mm"], 1)

            steps(pe, NG, router)

            def xn2_turn(i):
                for j in range(TG):
                    t = TG * i + j
                    wait(pe, "xn2_made", t + 1)
                    wait(pe, "xn2_out", t if j == 0 else t - 1)
                    for k in range(KD):
                        m = nc.tensor.transpose(bank[j % 2][:, k * P:(k + 1) * P], ytok[:, j, k * P:(k + 1) * P], ident[:, :])
                    m.then_inc(S["xn2_turned"], 1)

            pe.wait_ge(S["y_out"], NT)
            steps(pe, NG, xn2_turn)
            pe.wait_ge(S["gates_made"], 1)
            pe.wait_ge(S["xn2_out"], NT)
            for t in range(NT):
                if t >= 2:
                    pe.wait_ge(S["b2_add"], t - 1)
                nc.tensor.transpose(bank[t % 2][0:EXP, 0:P], gate[:, t, :], ident[:, :]).then_inc(S["gate_turned"], 1)
                pe.wait_ge(S["gate_out"], t + 1)
                nc.tensor.matmul(bank[2 + t % 2][:, 0:D], gateT[0:EXP, t % 2, :], b2_sb[0:EXP, :], start=True, stop=True).then_inc(S["b2_mm"], 1)
            pe.wait_ge(S["b2_add"], NT)

            def fold(e):
                pe.wait_ge(s_w[e % 2], 32 * (e // 2 + 1))
                if e >= 1:
                    pe.wait_ge(S["fold_b"], e)
                for q in range(HC):
                    for k in range(KD):
                        m = nc.tensor.matmul(bank[6][:, q:q + 1], w1s[e % 2][:, k, q * P:(q + 1) * P], bcols[:, e, k:k + 1],
                                             start=k == 0, stop=k == KD - 1)
                m.then_inc(S["fold_mm"], 1)

            fold(0)
            tiles_of = ((0, 1, 2), (3, 4))
            for e in range(EXP):
                pe.wait_ge(S["fold_w"], KD * (e + 1))

                def experts(i):
                    for h in range(2):
                        for q in range(HC):
                            n = (e * NG * 2 + h) * HC + q + i * 2 * HC
                            wait(pe, "hid_act", n - 1 if q < 2 else n - 2)
                            for k in range(KD):
                                m = nc.tensor.matmul(bank[q % 3][:, 0:HTOK], w1s[e % 2][:, k, q * P:(q + 1) * P],
                                                     hT_all[:, k, bass.ds(TOK * i + HTOK * h, HTOK)], start=k == 0, stop=k == KD - 1)
                            m.then_inc(S["hid_mm"], 1)
                    for j in range(TG):
                        n = NT * e + TG * i + j
                        wait(pe, "hid_act", (e * NG * 2 + (1 if j < 2 else 2)) * HC + i * 2 * HC)
                        wait(pe, "out_acc", n - 1 if j < 2 else n - 2)
                        segs = token_parts(j)
                        for q in range(HC):
                            for (h, a, b, r) in segs:
                                m = nc.tensor.matmul(bank[3 + j % 3][r:r + b - a, 0:D], hid[h][:, q, a:b], w2s[e % 2][:, q, :],
                                                     start=q == 0, stop=q == HC - 1)
                        m.then_inc(S["out_mm"], 1)

                experts(0)
                if e + 1 < EXP:
                    fold(e + 1)
                with pe.Fori(1, NG) as i:
                    experts(i)


def token_parts(j):
    a, b = j * P, (j + 1) * P
    if b <= HTOK:
        return [(0, a, b, 0)]
    if a >= HTOK:
        return [(1, a - HTOK, b - HTOK, 0)]
    return [(0, a, HTOK, 0), (1, 0, b - HTOK, HTOK - a)]


_INS = ["x", "src", "dst", "edge_type_8", "L0_gnn_weights", "L0_gnn_roots", "L0_gnn_biases", "L0_mix_W_qkv",
        "L0_mix_W_out", "L0_mix_b_out", "L0_ffn_Wr", "L0_ffn_br", "L0_ffn_ln_g", "L0_ffn_ln_b",
        "L0_ffn_W1", "L0_ffn_b1", "L0_ffn_W2", "L0_ffn_b2"]


def kernel(**inputs):
    import numpy as _np
    import concourse.bacc as _bacc
    from concourse import mybir as _mybir
    from concourse.bass_utils import run_bass_kernel_spmd as _run

    nc = _bacc.Bacc("TRN2", target_bir_lowering=False, num_devices=1)
    arrays, args = {}, []
    for name in _INS:
        a = _np.ascontiguousarray(inputs[name])
        arrays[f"in_{name}_dram"] = a
        args.append(nc.dram_tensor(f"in_{name}_dram", a.shape, _mybir.dt.from_np(a.dtype), kind="ExternalInput").ap())
    args.append(nc.dram_tensor("out_0_dram", (N_NODES, D), _mybir.dt.float32, kind="ExternalOutput").ap())
    gps_layer(nc, *args)
    r = _run(nc, [arrays], core_ids=[0])
    return r.results[0]["out_0_dram"]
```

```python
import concourse.bass as bass
from concourse import mybir
from contextlib import ExitStack

F32 = mybir.dt.float32
I32 = mybir.dt.int32
U32 = mybir.dt.uint32
ALU = mybir.AluOpType
ACT = mybir.ActivationFunctionType
AXX = mybir.AxisListType.X

P = 128
N_NODES, D = 3125, 256
KD = D // P
NT = -(-N_NODES // P)
NP = NT * P
LAST = N_NODES - (NT - 1) * P
TG = 5
NG = NT // TG
REL, LAYERS = 8, 3
EDGES = 103125
WIN = 64
GWIN = 400
NGW = NP // GWIN
HALF = 5
STEP = 2 * HALF
REAL_TILES = -(-EDGES // P)
STEPS = -(-REAL_TILES // STEP)
ETILES = STEPS * STEP
EC = -(-ETILES // P)
FULL_C = EDGES // (P * P)
FULL_R = (EDGES - FULL_C * P * P) // P
REST = EDGES - FULL_C * P * P - FULL_R * P
NO_NODE = 8192.0
HEADS, DH = 4, 32
HID = HEADS * DH
NCH = 8
EXP, HF = 8, 1024
HC = HF // P
TOK = TG * P
TOPK = 2
SLOT_T = (TOPK * N_NODES + EXP * (P - 1)) // P
SLOT_T += SLOT_T % 2
SLOTS = SLOT_T * P
XS_T = SLOT_T + 2
EPS = 1e-5
ARENA = 38300
FFW = 2 * EXP + 3


def gps_layer(nc, x, src, dst, etype, gw, groots, gbias, wqkv, wout, bout,
              Wr, br, ln_g, ln_b, W1, b1, W2, b2, out):
    ctx = ExitStack()
    with ctx:
        ctx.enter_context(nc.allow_non_contiguous_dma(reason="short bias and window columns"))

        def sb(name, shape, dt=F32):
            return ctx.enter_context(nc.sbuf_tensor(name, shape, dt))

        y_dram = [nc.dram_tensor(f"y_dram{i}", (NP * REL, D), F32).ap() for i in range(2)]
        xs_dram = nc.dram_tensor("xs_dram", (XS_T * P, D), F32).ap()
        ys_dram = nc.dram_tensor("ys_dram", (XS_T * P, D), F32).ap()
        b1_dram = nc.dram_tensor("b1_dram", (EXP, HF), F32).ap()
        win_dram = nc.dram_tensor("win_dram", (EC * P,), I32).ap()

        xtok = sb("xtok", [P, NT, D])
        hT_all = sb("hT_all", [P, KD, NP])
        ident = sb("ident", [P, P])
        ones = sb("ones", [P, P])
        zcol = sb("zcol", [P, 1])
        iota_w = sb("iota_w", [P, GWIN])
        stats = sb("stats", [P, NT, 6])
        mv = sb("mv", [P, NT, 2])
        rstd = sb("rstd", [P, NT])
        mv2 = sb("mv2", [P, NT, 2])
        rstd2 = sb("rstd2", [P, NT])
        zrow = sb("zrow", [P, D])
        tri = sb("tri", [P, P])
        node_in = sb("node_in", [P, NT])
        pad_pos = sb("pad_pos", [P, TOPK, NT])
        pos = sb("pos", [P, TOPK, NT], I32)
        flag = sb("flag", [P, 1], I32)
        arena = sb("arena", [P, ARENA])
        used = [0]

        def carve(n):
            a = arena[:, used[0]:used[0] + n]
            used[0] += n
            assert used[0] <= ARENA, used[0]
            return a

        idx_i = carve(EC * P).bitcast(I32)
        dloc = carve(EC * P)
        dabs = carve(EC * P)
        win_row = carve(EC * P).bitcast(I32)
        bias_g = carve(LAYERS * KD).rearrange("p (l k) -> p l k", l=LAYERS)
        wrel = carve(KD * REL * D).rearrange("p (k n) -> p k n", k=KD)
        wroot = carve(KD * D).rearrange("p (k n) -> p k n", k=KD)
        ybuf = carve(4 * 512).rearrange("p (c n) -> p c n", c=4)
        stage = carve(TG * KD * P).rearrange("p (c k n) -> p c k n", c=TG, k=KD)
        gath = carve(STEP * D).rearrange("p (c n) -> p c n", c=STEP)
        onehot = carve(STEP * WIN).rearrange("p (c n) -> p c n", c=STEP)
        ghot = carve(GWIN)
        gcol = carve(2)
        idx_ring = carve(STEP).bitcast(I32)
        xnt = carve(TG * D).rearrange("p (c n) -> p c n", c=TG)
        wqkv_sb = carve(KD * 3 * HID).rearrange("p (k n) -> p k n", k=KD)
        wout_sb = carve(D)
        bout_sb = carve(D)
        mark = used[0]
        e_src = carve(EC * P).bitcast(I32).rearrange("p (c n) -> p c n", c=EC)
        e_dst = carve(EC * P).bitcast(I32).rearrange("p (c n) -> p c n", c=EC)
        e_typ = carve(EC * P).bitcast(I32).rearrange("p (c n) -> p c n", c=EC)
        e_dstf = carve(EC * P).rearrange("p (c n) -> p c n", c=EC)
        e_idx = carve(EC * P).rearrange("p (c n) -> p c n", c=EC)
        e_loc = carve(EC * P).rearrange("p (c n) -> p c n", c=EC)
        e_in = carve(EC * P).rearrange("p (c n) -> p c n", c=EC)
        e_win = carve(EC)
        e_wini = carve(EC).bitcast(I32)
        e_viol = carve(1)
        used[0] = mark
        qT = carve(NP)
        kT = carve(NP)
        vtok = carve(NP).rearrange("p (t n) -> p t n", t=NT)
        ktok = carve(2 * P).rearrange("p (c n) -> p c n", c=2)
        nkmax = carve(1)
        ksum = carve(1)
        krec = carve(1)
        ctxT = carve(P)
        mctx = carve(D)
        used[0] = 0
        w2a = carve(EXP * HC * D).rearrange("p (q e n) -> p q (e n)", e=EXP, q=HC)
        w1a = carve(EXP * KD * HF).rearrange("p (k e n) -> p k (e n)", e=EXP, k=KD)
        gcols = carve(EXP * KD).rearrange("p (e k) -> p e k", e=EXP)
        bcols = carve(EXP * KD).rearrange("p (e k) -> p e k", e=EXP)
        bsel = carve(EXP * KD * EXP).rearrange("p (e k f) -> p e k f", e=EXP, k=KD)
        b1_sb = carve(HF)
        xnt_b1 = b1_sb
        wr_sb = carve(KD * EXP).rearrange("p (k n) -> p k n", k=KD)
        br_sb = carve(EXP)
        lg = carve(NT * EXP).rearrange("p (t e) -> p t e", t=NT)
        pr = carve(NT * EXP).rearrange("p (t e) -> p t e", t=NT)
        hit = [carve(NT * EXP).rearrange("p (t e) -> p t e", t=NT) for _ in range(TOPK)]
        chosen = carve(NT * EXP).rearrange("p (t e) -> p t e", t=NT)
        top = carve(NT * 8).rearrange("p (t e) -> p t e", t=NT)
        topi = carve(NT * 8).bitcast(U32).rearrange("p (t e) -> p t e", t=NT)
        topf = pr
        rmax = carve(NT)
        rsum = carve(NT)
        rrec = carve(NT)
        cnt_i = carve(EXP).bitcast(I32)
        ntl = carve(EXP)
        tend = carve(EXP)
        sbase = carve(EXP)
        slot_exp = carve(XS_T).bitcast(I32)
        slot_expf = carve(XS_T)
        spos = carve(NT)
        ytok = carve(TG * D).rearrange("p (c n) -> p c n", c=TG)
        yT = carve(TG * KD * P).rearrange("p (c k n) -> p c k n", c=TG, k=KD)
        used[0] -= TG * KD * P
        before = carve(NT * EXP).rearrange("p (t e) -> p t e", t=NT)
        tile_cnt = carve(EXP * NT).rearrange("p (e t) -> p e t", t=NT)
        upto = carve(EXP * NT).rearrange("p (e t) -> p e t", t=NT)
        past = carve(XS_T * EXP).rearrange("p (s e) -> p s e", s=XS_T)
        xrow = hT_all[:, :, :].rearrange("p k n -> p (k n)").rearrange("p (t d) -> p t d", d=D)
        hflat = hT_all[:, :, :].rearrange("p k n -> p (k n)")
        hrow = hflat[:, 0:HF]
        hTq = hflat[:, HF:2 * HF].rearrange("p (q n) -> p q n", q=HC)
        b1t = [hflat[:, (2 + i) * HF:(3 + i) * HF] for i in range(2)]
        b2t = [hflat[:, 4 * HF + i * D:4 * HF + (i + 1) * D] for i in range(2)]
        xs = [ytok[:, i, :] for i in range(2)]
        orow = [ytok[:, 2 + i, :] for i in range(2)]
        xsT = [yT[:, i, :, :] for i in range(2)]
        back = [w2a[:, q, 0:TG * D].rearrange("p (j d) -> p j d", j=TG) for q in range(4)]

        bank = [ctx.enter_context(nc.psum_tensor(f"bank{i}", [P, 512], F32)) for i in range(8)]

        names = """x_in edge_in gb_in wrel_in mixw_in ffw_in win_out win_in out_st
            const pads edges_made edge_turned edge_back viol_sum flag_set
            var_made sd_made rstd_made xn_made xn_turned stage_full
            y_mm y_act y_dve node_mm root_out qkv_out
            ix_ready tile_mm hot_ready tile_add gen_hot gen_mm gen_add layer_done
            kmax_made kexp_made k_turned k_out ctx_mm ctx_out mctx_mm mctx_out mix_mm mix_add
            sg_made sg_turned sg_add y_made y_stats y_turned y_out xn2_made
            router_mm router_in router_exp b1_mm b1_out b1_st sel_made sel_mm slots_made w_scaled bsel_made zero_st
            scat_st xs_turned xs_back hid_mm hid_pre hid_act hid_turned hid_back_v hid_back_s out_mm out_back
            combined chain_v""".split()
        S = {n: ctx.enter_context(nc.semaphore(n)) for n in names}
        s_gath = [ctx.enter_context(nc.semaphore(f"gath{j}")) for j in range(STEP)]
        s_yst = [ctx.enter_context(nc.semaphore(f"y_stored{c}")) for c in range(4)]
        s_wexp = [ctx.enter_context(nc.semaphore(f"w{c}_in")) for c in (1, 2)]
        s_xs = [ctx.enter_context(nc.semaphore(f"xs_in{c}")) for c in range(2)]
        s_bias = [ctx.enter_context(nc.semaphore(f"bias_in{c}")) for c in range(2)]
        s_ys = [ctx.enter_context(nc.semaphore(f"ys_out{c}")) for c in range(2)]
        s_back = [ctx.enter_context(nc.semaphore(f"back_in{c}")) for c in range(4)]
        block = ctx.enter_context(nc.Block())

        def wait(eng, s, v):
            if isinstance(v, int) and v <= 0:
                return
            eng.wait_ge(S[s] if isinstance(s, str) else s, v)

        def wait_apart(eng, s, v):
            wait(eng, s, v)
            eng.nop(nofuse=True)

        def steps(eng, n, body):
            body(0)
            with eng.Fori(1, n) as i:
                body(i)

        def tile_of(a, t):
            return a[:, bass.ds(t, 1), :].rearrange("p o n -> p (o n)")

        w_rel = gw.rearrange("l r (k p) n -> l p k r n", p=P)
        w_root = groots.rearrange("l (k p) n -> l p k n", p=P)

        @block.sync
        def _(sp):
            sp.dma_start(xtok[:, 0:NT - 1, :], x[0:(NT - 1) * P, :].rearrange("(t p) d -> p t d", p=P)).then_inc(S["x_in"], 16)
            sp.wait_ge(S["pads"], 1)
            sp.dma_start(xtok[0:LAST, NT - 1, :], x[(NT - 1) * P:N_NODES, :]).then_inc(S["x_in"], 16)

            def layer_weights(l):
                for k in range(KD):
                    sp.dma_start(wrel[:, k, :].rearrange("p (r n) -> p r n", r=REL), w_rel[l][:, k]).then_inc(S["wrel_in"], 16)
                sp.dma_start(wroot, w_root[l]).then_inc(S["wrel_in"], 16)

            layer_weights(0)
            sp.wait_ge(S["const"], 8)
            sp.dma_start(xs_dram.rearrange("(t p) d -> p t d", p=P), zrow[:, :].unsqueeze(1).to_broadcast([P, XS_T, D])).then_inc(S["zero_st"], 16)
            sp.dma_start(ys_dram[SLOTS:XS_T * P, :].rearrange("(t p) d -> p t d", p=P), zrow[:, :].unsqueeze(1).to_broadcast([P, TOPK, D])).then_inc(S["zero_st"], 16)
            sp.wait_ge(S["pads"], 4)
            at0, at1 = FULL_C * P * P, FULL_C * P * P + FULL_R * P
            for a, e in ((src, e_src), (dst, e_dst), (etype, e_typ)):
                sp.dma_start(e[:, 0:FULL_C, :], a[0:at0].rearrange("(c p l) -> p c l", p=P, l=P)).then_inc(S["edge_in"], 16)
                sp.dma_start(e[0:FULL_R, FULL_C, :], a[at0:at1].rearrange("(p l) -> p l", l=P)).then_inc(S["edge_in"], 16)
                sp.dma_start(e[FULL_R:FULL_R + 1, FULL_C, 0:REST], a[at1:EDGES].rearrange("(p l) -> p l", p=1)).then_inc(S["edge_in"], 16)
            sp.dma_start(wqkv_sb, wqkv.rearrange("(k p) n -> p k n", p=P)).then_inc(S["mixw_in"], 16)
            sp.dma_start(wout_sb, wout).then_inc(S["mixw_in"], 16)
            sp.dma_start(bout_sb[0:1, :], bout.rearrange("(o n) -> o n", o=1)).then_inc(S["mixw_in"], 16)
            for l in range(LAYERS):
                sp.dma_start(bias_g[:, l, :], gbias[l].rearrange("(k p) -> p k", p=P)).then_inc(S["gb_in"], 16)
            sp.wait_ge(S["edges_made"], 1)
            sp.dma_start(win_dram.rearrange("(c p) -> p c", p=P), e_wini).then_inc(S["win_out"], 16)
            sp.wait_ge(S["win_out"], 16)
            sp.dma_start(win_row[0:1, :], win_dram.rearrange("(o n) -> o n", o=1)).then_inc(S["win_in"], 16)

            for l in range(LAYERS):
                yd = y_dram[l % 2].rearrange("(t p r) d -> p t (r d)", p=P, r=REL)

                def store(t):
                    for c in range(4):
                        wait(sp, "y_act" if c % 2 == 0 else "y_dve", 2 * NT * l + 2 * t + c // 2 + 1)
                        sp.dma_start(yd[:, bass.ds(t, 1), c * 512:(c + 1) * 512].rearrange("p o n -> p (o n)"),
                                     ybuf[:, c, :]).then_inc(s_yst[c], 16)

                steps(sp, NT, store)
                if l + 1 < LAYERS:
                    sp.wait_ge(S["node_mm"], NT * (l + 1))
                    layer_weights(l + 1)
            for c in range(4):
                sp.wait_ge(s_yst[c], 16 * NT * LAYERS)

            sp.wait_ge(S["node_mm"], NT * LAYERS)
            for k in range(KD):
                sp.dma_start(w1a[:, k, :].rearrange("p (e n) -> p e n", e=EXP),
                             W1.rearrange("e (k p) n -> k p e n", p=P)[k]).then_inc(s_wexp[0], 16)
            for a, b in ((gcols, ln_g.rearrange("e (k p) -> p e k", p=P)), (bcols, ln_b.rearrange("e (k p) -> p e k", p=P))):
                for e in range(EXP):
                    sp.dma_start(a[:, e, :], b[:, e, :]).then_inc(S["ffw_in"], 16)
            sp.dma_start(wr_sb, Wr.rearrange("(k p) n -> p k n", p=P)).then_inc(S["ffw_in"], 16)
            sp.dma_start(br_sb[0:1, :], br.rearrange("(o n) -> o n", o=1)).then_inc(S["ffw_in"], 16)
            sp.dma_start(b1_sb[0:EXP, :], b1).then_inc(S["ffw_in"], 16)
            sp.wait_ge(S["layer_done"], LAYERS)
            for q in range(HC):
                sp.dma_start(w2a[:, q, :].rearrange("p (e n) -> p e n", e=EXP),
                             W2.rearrange("e (q p) n -> q p e n", p=P)[q]).then_inc(s_wexp[1], 16)
            sp.wait_ge(S["b1_out"], 2)
            sp.dma_start(b1_dram, xnt_b1[0:EXP, :]).then_inc(S["b1_st"], 16)
            sp.wait_ge(S["b1_st"], 16)
            sp.wait_ge(S["slots_made"], 2)
            sp.wait_ge(S["scat_st"], 16 * TOPK * NT)

            def load_rows(s, c):
                sp.dma_start(xs[c], xs_dram.rearrange("(t p) d -> p t d", p=P)[:, bass.ds(s, 1), :].rearrange("p o d -> p (o d)")).then_inc(s_xs[c], 16)

            def load_bias(s, c):
                e = sp.value_load(slot_exp[0:1, bass.ds(s, 1)], min_val=0, max_val=EXP - 1)
                sp.dma_start(b1t[c], b1_dram[bass.ds(e, 1), :].to_broadcast([P, HF])).then_inc(s_bias[c], 16)
                sp.dma_start(b2t[c], b2[bass.ds(e, 1), :].to_broadcast([P, D])).then_inc(s_bias[c], 16)

            for c in range(2):
                load_rows(c, c)
                load_bias(c, c)

            def feed(i):
                for c in range(2):
                    s = 2 * i + c
                    sp.wait_ge(S["xs_turned"], s + 1)
                    load_rows(s + 2, c)
                for c in range(2):
                    s = 2 * i + c
                    sp.wait_ge(S["out_back"], s + 1)
                    sp.dma_start(ys_dram[0:SLOTS, :].rearrange("(t p) d -> p t d", p=P)[:, bass.ds(s, 1), :].rearrange("p o d -> p (o d)"), orow[c]).then_inc(s_ys[c], 16)
                    load_bias(s + 2, c)

            feed(0)
            with sp.Fori(1, SLOT_T // 2) as i:
                feed(i)
            for c in range(2):
                sp.wait_ge(s_ys[c], 16 * (SLOT_T // 2))
                sp.wait_ge(s_xs[c], 16 * (SLOT_T // 2 + 1))
                sp.wait_ge(s_bias[c], 32 * (SLOT_T // 2 + 1))
            for g in range(NG):
                sp.wait_ge(S["combined"], TOPK * TG * (g + 1))
                if g < NG - 1:
                    sp.dma_start(out[g * TOK:(g + 1) * TOK, :].rearrange("(t p) d -> p t d", p=P), xtok[:, g * TG:(g + 1) * TG, :]).then_inc(S["out_st"], 16)
                else:
                    sp.dma_start(out[g * TOK:(NT - 1) * P, :].rearrange("(t p) d -> p t d", p=P), xtok[:, g * TG:NT - 1, :]).then_inc(S["out_st"], 16)
                    sp.dma_start(out[(NT - 1) * P:N_NODES, :], xtok[0:LAST, NT - 1, :]).then_inc(S["out_st"], 16)
            sp.wait_ge(S["out_st"], 16 * (NG + 1))

        @block.gpsimd
        def _(pool):
            nc.gpsimd.memset(xtok[:, NT - 1, :], 0.0).then_inc(S["pads"], 1)
            nc.gpsimd.memset(e_src, 0).then_inc(S["pads"], 1)
            nc.gpsimd.memset(e_typ, 0).then_inc(S["pads"], 1)
            nc.gpsimd.memset(e_dst, int(NO_NODE)).then_inc(S["pads"], 1)
            nc.gpsimd.memset(ones[:, :], 1.0).then_inc(S["const"], 1)
            nc.gpsimd.iota(iota_w[:, :], [[1, GWIN]], base=0, channel_multiplier=0,
                           allow_small_or_imprecise_dtypes=True).then_inc(S["const"], 1)
            nc.gpsimd.memset(zrow[:, :], 0.0).then_inc(S["const"], 1)
            nc.gpsimd.memset(tri[:, :], 1.0).then_inc(S["const"], 1)
            nc.gpsimd.iota(pad_pos[:, 0, :], [[P, NT]], base=0, channel_multiplier=1,
                           allow_small_or_imprecise_dtypes=True).then_inc(S["const"], 1)
            nc.gpsimd.memset(ident[:, :], 0.0).then_inc(S["const"], 1)
            pool.wait_ge(S["const"], 6)
            nc.gpsimd.affine_select(out=tri[:, :], in_=tri[:, :], compare_op=ALU.is_gt, fill=0.0, base=0,
                                    pattern=[[1, P]], channel_multiplier=-1).then_inc(S["const"], 1)
            nc.gpsimd.affine_select(out=ident[:, :], in_=ident[:, :], compare_op=ALU.not_equal, fill=1.0, base=0,
                                    pattern=[[-1, P]], channel_multiplier=1).then_inc(S["const"], 1)
            for l in range(LAYERS):
                for c in range(4):
                    pool.wait_ge(s_yst[c], 16 * NT * (l + 1))
                yd = y_dram[l % 2]

                def gather(i):
                    for h in range(2):
                        wait(pool, "ix_ready", 2 * STEPS * l + 2 * i + h + 1)
                        pool.nop(nofuse=True)
                        for j in range(h * HALF, h * HALF + HALF):
                            nc.gpsimd.indirect_dma_start(
                                out=gath[:, j, :], out_offset=None, in_=yd,
                                in_offset=bass.IndirectOffsetOnAxis(ap=idx_ring[:, j:j + 1], axis=0)).then_inc(s_gath[j], 16)

                steps(pool, STEPS, gather)
            pool.wait_ge(S["zero_st"], 32)
            pool.wait_ge(S["slots_made"], 1)
            for t in range(NT):
                for c in range(TOPK):
                    nc.gpsimd.indirect_dma_start(out=xs_dram, out_offset=bass.IndirectOffsetOnAxis(ap=pos[:, c, t:t + 1], axis=0),
                                                 in_=xrow[:, t, :], in_offset=None).then_inc(S["scat_st"], 16)
            for c in range(2):
                pool.wait_ge(s_ys[c], 16 * (SLOT_T // 2))
            for g in range(NG):
                for c in range(TOPK):
                    b = (2 * g + c) % 4
                    if g >= 2:
                        pool.wait_ge(S["combined"], TOPK * TG * (g - 1))
                    for j in range(TG):
                        nc.gpsimd.indirect_dma_start(out=back[b][:, j, :], out_offset=None, in_=ys_dram,
                                                     in_offset=bass.IndirectOffsetOnAxis(ap=pos[:, c, g * TG + j:g * TG + j + 1], axis=0)).then_inc(s_back[b], 16)

        @block.scalar
        def _(act):
            act.wait_ge(S["var_made"], 1)
            nc.scalar.activation(rstd[:, :], mv[:, :, 1], ACT.Sqrt).then_inc(S["sd_made"], 1)
            for b, (o, n0, n1) in enumerate(((idx_i, 0, 4), (idx_i, 4, EC), (dloc, 0, 4), (dloc, 4, EC), (dabs, 0, 4), (dabs, 4, EC))):
                act.wait_ge(S["edge_turned"], b + 1)
                nc.scalar.copy(o[:, n0 * P:n1 * P], bank[b][:, 0:(n1 - n0) * P]).then_inc(S["edge_back"], 1)
            act.wait_ge(S["gb_in"], 16 * LAYERS)
            for l in range(LAYERS):
                if l > 0:
                    act.wait_ge(S["layer_done"], l)

                def node_out(i):
                    if l > 0:
                        for j in range(TG):
                            t = TG * i + j
                            wait_apart(act, "node_mm", NT * l + t + 1 - TG)
                            nc.scalar.activation(stage[:, j, :, :], hT_all[:, :, bass.ds(TOK * i + P * j, P)],
                                                 ACT.Relu).then_inc(S["stage_full"], 1)
                    else:
                        for j in range(TG):
                            t = TG * i + j
                            wait(act, "xn_turned", t + 1)
                            wait(act, "node_mm", t + 1 - TG)
                            nc.scalar.copy(stage[:, j, :, :], bank[6 + j % 2][:, 0:D].rearrange("p (k n) -> p k n", k=KD)).then_inc(S["stage_full"], 1)
                    for j in range(TG):
                        t = TG * i + j
                        for c in (0, 2):
                            wait(act, "y_mm", 4 * NT * l + 4 * t + c + 1)
                            wait(act, s_yst[c], 16 * (NT * l + t))
                            nc.scalar.copy(ybuf[:, c, :], bank[c][:, :]).then_inc(S["y_act"], 1)
                        wait_apart(act, "node_mm", NT * l + t + 1)
                        for e in range(KD):
                            nc.scalar.activation(hT_all[:, e, bass.ds(TOK * i + P * j, P)], bank[4][:, e * P:(e + 1) * P],
                                                 ACT.Identity, bias=bias_g[:, l, e:e + 1]).then_inc(S["root_out"], 1)

                steps(act, NG, node_out)
                if l == 0:
                    act.wait_ge(S["kmax_made"], 1)
                    nc.scalar.activation(kT[:, 0:N_NODES], kT[:, 0:N_NODES], ACT.Exp, bias=nkmax, accum_out=ksum).then_inc(S["kexp_made"], 1)

                def ring(i):
                    for h in range(2):
                        wait(act, "tile_mm", ETILES * l + STEP * i + HALF * (h - 1))
                        nc.scalar.copy(idx_ring[:, h * HALF:(h + 1) * HALF],
                                       idx_i[:, bass.ds(STEP * i + h * HALF, HALF)]).then_inc(S["ix_ready"], 1)

                steps(act, STEPS, ring)
            act.wait_ge(S["layer_done"], LAYERS)

            def sigmoid(i):
                for j in range(TG):
                    wait_apart(act, "sg_turned", TG * i + j + 1 - TG)
                    nc.scalar.activation(yT[:, j, :, :], hT_all[:, :, bass.ds(TOK * i + P * j, P)], ACT.Sigmoid).then_inc(S["sg_made"], 1)

            steps(act, NG, sigmoid)
            act.wait_ge(S["var_made"], 2)
            nc.scalar.activation(rstd[:, :], mv[:, :, 1], ACT.Sqrt).then_inc(S["sd_made"], 1)
            act.wait_ge(S["sg_turned"], NT)

            def y_back(i):
                for j in range(TG):
                    t = TG * i + j
                    wait(act, "y_turned", t + 1)
                    wait(act, "router_mm", t + 1 - TG)
                    nc.scalar.copy(yT[:, j, :, :], bank[j % 2][:, 0:D].rearrange("p (k n) -> p k n", k=KD)).then_inc(S["y_out"], 1)

            steps(act, NG, y_back)
            act.wait_ge(S["var_made"], 3)
            nc.scalar.activation(rstd2[:, :], mv2[:, :, 1], ACT.Sqrt).then_inc(S["sd_made"], 1)

            act.wait_ge(S["router_in"], 1)
            nc.scalar.activation(pr, lg, ACT.Exp).then_inc(S["router_exp"], 1)
            act.wait_ge(S["b1_mm"], 1)
            for e in range(EXP):
                nc.scalar.activation(w1a[:, 1, e * HF:(e + 1) * HF], w1a[:, 1, e * HF:(e + 1) * HF], ACT.Copy,
                                     scale=gcols[:, e, 1:2]).then_inc(S["w_scaled"], 1)

            def rows_back(n, c):
                act.wait_ge(S["xs_turned"], n + 1)
                nc.scalar.copy(xsT[c], bank[0][:, 0:D].rearrange("p (k n) -> p k n", k=KD)).then_inc(S["xs_back"], 1)

            rows_back(0, 0)
            rows_back(1, 1)

            def slot(i):
                for c in range(2):
                    s = 2 * i + c
                    for h in range(2):
                        act.wait_ge(S["hid_pre"], 2 * s + h + 1)
                        nc.scalar.activation(hrow[:, h * 512:(h + 1) * 512], hrow[:, h * 512:(h + 1) * 512], ACT.Gelu).then_inc(S["hid_act"], 1)
                    act.wait_ge(S["hid_turned"], 2 * s + 2)
                    nc.scalar.copy(hTq[:, HC // 2:HC, :], bank[4][:, :].rearrange("p (q n) -> p q n", q=HC // 2)).then_inc(S["hid_back_s"], 1)
                    rows_back(s + 2, c)

            slot(0)
            with act.Fori(1, SLOT_T // 2) as i:
                slot(i)

        @block.vector
        def _(dve):
            chain = [0]

            def link(ins):
                chain[0] += 1
                ins.then_inc(S["chain_v"], 1)
                dve.wait_ge(S["chain_v"], chain[0])

            def fence():
                link(nc.vector.memset(zcol[:, :], 0.0))

            def row_stats(rows):
                with dve.Fori(0, NT) as t:
                    nc.vector.bn_stats(tile_of(stats, t), tile_of(rows, t))
                fence()
                for t in range(NT):
                    nc.vector.bn_aggr(mv[:, t, :], stats[:, t, :])
                fence()
                nc.vector.tensor_scalar(mv[:, :, 1], mv[:, :, 1], EPS, None, ALU.add).then_inc(S["var_made"], 1)

            dve.wait_ge(S["const"], 8)
            link(nc.vector.tensor_scalar(node_in[:, :], pad_pos[:, 0, :], float(N_NODES), None, ALU.is_lt))
            link(nc.vector.tensor_scalar(rstd2[:, :], node_in[:, :], -1.0, 1.0, ALU.mult, ALU.add))
            link(nc.vector.tensor_scalar(pad_pos[:, 1, :], pad_pos[:, 0, :], float(SLOTS + P - (NT - 1) * P), None, ALU.add))
            link(nc.vector.tensor_scalar(pad_pos[:, 0, :], pad_pos[:, 0, :], float(SLOTS - (NT - 1) * P), None, ALU.add))
            link(nc.vector.tensor_tensor(pad_pos[:, :, :], pad_pos[:, :, :], rstd2[:, :].unsqueeze(1).to_broadcast([P, TOPK, NT]), ALU.mult))
            dve.wait_ge(S["x_in"], 32)
            row_stats(xtok)
            dve.wait_ge(S["edge_in"], 9 * 16)
            link(nc.vector.tensor_copy(e_dstf, e_dst))
            nc.vector.scalar_tensor_tensor(out=e_idx, in0=e_src, scalar=float(REL), in1=e_typ, op0=ALU.mult, op1=ALU.add)
            link(nc.vector.tensor_reduce(out=e_win, in_=e_dstf, op=ALU.min, axis=AXX))
            link(nc.vector.tensor_scalar(e_win, e_win, float(NP - WIN), None, ALU.min))
            nc.vector.tensor_copy(e_wini, e_win).then_inc(S["edges_made"], 1)
            link(nc.vector.tensor_tensor(e_loc, e_dstf, e_win.unsqueeze(2).to_broadcast([P, EC, P]), ALU.subtract))
            nc.vector.memset(zcol[:, :], 0.0).then_inc(S["edges_made"], 1)
            link(nc.vector.tensor_scalar(e_in, e_dstf, NO_NODE / 2, None, ALU.is_lt))
            link(nc.vector.scalar_tensor_tensor(out=e_in, in0=e_loc, scalar=float(WIN), in1=e_in, op0=ALU.is_ge, op1=ALU.mult))
            nc.vector.tensor_reduce(out=e_viol, in_=e_in.rearrange("p c n -> p (c n)"), op=ALU.add, axis=AXX).then_inc(S["edges_made"], 1)
            dve.wait_ge(S["viol_sum"], 1)
            nc.vector.tensor_scalar(flag[:, :], bank[6][:, 0:1], 1.0, None, ALU.min).then_inc(S["flag_set"], 1)
            dve.wait_ge(S["sd_made"], 1)
            link(nc.vector.reciprocal(rstd[:, :], rstd[:, :]))

            for l in range(LAYERS):
                def node_out(i):
                    if l == 0:
                        for j in range(TG):
                            t = TG * i + j
                            wait(dve, "xn_turned", t + 1 - TG)
                            nc.vector.tensor_scalar(xnt[:, j, :], tile_of(xtok, t), mv[:, bass.ds(t, 1), 0],
                                                    rstd[:, bass.ds(t, 1)], ALU.subtract, ALU.mult).then_inc(S["xn_made"], 1)
                    for j in range(TG):
                        t = TG * i + j
                        for c in (1, 3):
                            wait(dve, "y_mm", 4 * NT * l + 4 * t + c + 1)
                            wait(dve, s_yst[c], 16 * (NT * l + t))
                            nc.vector.tensor_copy(ybuf[:, c, :], bank[c][:, :]).then_inc(S["y_dve"], 1)
                        if l == 0:
                            wait(dve, "node_mm", t + 1)
                            nc.vector.tensor_copy(qT[:, bass.ds(TOK * i + P * j, P)], bank[5][:, 0:P])
                            nc.vector.tensor_copy(kT[:, bass.ds(TOK * i + P * j, P)], bank[5][:, P:2 * P])
                            nc.vector.tensor_copy(tile_of(vtok, t), bank[5][:, 2 * P:3 * P]).then_inc(S["qkv_out"], 1)

                steps(dve, NG, node_out)
                if l == 0:
                    fence()
                    link(nc.vector.reduce_max(nkmax, kT[:, 0:N_NODES], AXX))
                    nc.vector.tensor_scalar(nkmax, nkmax, -1.0, None, ALU.mult).then_inc(S["kmax_made"], 1)
                    for t in range(NT):
                        dve.wait_ge(S["k_turned"], t + 1)
                        nc.vector.tensor_copy(ktok[:, t % 2, :], bank[t % 2][:, 0:P]).then_inc(S["k_out"], 1)
                    link(nc.vector.reciprocal(krec, ksum))
                    link(nc.vector.tensor_scalar(krec, krec, float(DH) ** -0.5, None, ALU.mult))
                    link(nc.vector.memset(ctxT, 0.0))
                    dve.wait_ge(S["ctx_mm"], NT)
                    for h in range(HEADS):
                        r = slice(h * DH, (h + 1) * DH)
                        last = nc.vector.tensor_copy(ctxT[r, r], bank[2][r, r])
                    last.then_inc(S["ctx_out"], 1)
                    dve.wait_ge(S["mctx_mm"], 1)
                    nc.vector.tensor_scalar(mctx, bank[3][:, 0:D], krec, None, ALU.mult).then_inc(S["mctx_out"], 1)
                    for t in range(NT):
                        dve.wait_ge(S["mix_mm"], t + 1)
                        nc.vector.tensor_tensor(xtok[:, t, :], xtok[:, t, :], bank[4 + t % 4][:, 0:D], ALU.add).then_inc(S["mix_add"], 1)
                    dve.wait_ge(S["win_in"], 16)
                    dve.wait_ge(S["edge_back"], 6)
                dve.wait_ge(S["root_out"], KD * NT * (l + 1))
                outside = dve.value_load(flag[0:1, 0:1], min_val=0, max_val=1)
                with dve.If(outside < 1):
                    def hot(i, h):
                        nc.vector.tensor_tensor(
                            onehot[:, h * HALF:(h + 1) * HALF, :],
                            iota_w[:, 0:WIN].unsqueeze(1).to_broadcast([P, HALF, WIN]),
                            dloc[:, bass.ds(STEP * i + h * HALF, HALF)].unsqueeze(2).to_broadcast([P, HALF, WIN]),
                            ALU.is_equal).then_inc(S["hot_ready"], 1)

                    hot(0, 0)
                    hot(0, 1)

                    def adds(i):
                        _, wins = nc.values_load_multi_w_load_instructions(
                            win_row[0:1, bass.ds(STEP * i, STEP)], engines=(dve.engine,), min_val=0, max_val=NP - WIN,
                            skip_runtime_bounds_check_because="clamped when they were made")
                        for h in range(2):
                            for j in range(h * HALF, h * HALF + HALF):
                                n = ETILES * l + STEP * i + j
                                wait(dve, "tile_mm", n + 1)
                                wait(dve, "tile_add", n)
                                a = hT_all[:, :, bass.ds(wins[j], WIN)]
                                nc.vector.tensor_tensor(a, a, bank[j % 2][:, 0:KD * WIN].rearrange("p (k n) -> p k n", k=KD),
                                                        ALU.add).then_inc(S["tile_add"], 1)
                            hot(i + 1, h)

                    steps(dve, STEPS, adds)
                    dve.wait_ge(S["tile_add"], ETILES * (l + 1))
                with dve.Else():
                    with dve.Fori(0, ETILES) as n:
                        nc.vector.tensor_copy(gcol[:, 0:1], dabs[:, bass.ds(n, 1)]).then_inc(S["gen_hot"], 1)
                        with dve.Fori(0, NGW) as v:
                            g = (n + ETILES * l) * NGW + v
                            dve.wait_ge(S["gen_hot"], (n + ETILES * l) * (2 * NGW + 1) + v * 2 + 1)
                            nc.vector.tensor_scalar(ghot, iota_w[:, :], gcol[:, 0:1], None, ALU.is_equal).then_inc(S["gen_hot"], 1)
                            dve.wait_ge(S["gen_hot"], (n + ETILES * l) * (2 * NGW + 1) + v * 2 + 2)
                            nc.vector.tensor_scalar(gcol[:, 0:1], gcol[:, 0:1], float(-GWIN), None, ALU.add).then_inc(S["gen_hot"], 1)
                            dve.wait_ge(S["gen_mm"], g + 1)
                            for k in range(KD):
                                a = hT_all[:, k, bass.ds(v * GWIN, GWIN)]
                                nc.vector.tensor_tensor(a, a, bank[k][:, 0:GWIN], ALU.add).then_inc(S["gen_add"], 1)
                            dve.wait_ge(S["gen_add"], (g + 1) * KD)
                nc.vector.memset(zcol[:, :], 0.0).then_inc(S["layer_done"], 1)

            dve.wait_ge(S["ffw_in"], 16 * FFW)
            link(nc.vector.memset(bsel, 0.0))
            for e in range(EXP):
                last = nc.vector.tensor_copy(bsel[:, e, :, e], bcols[:, e, :])
            last.then_inc(S["bsel_made"], 1)

            def gnn_add(i):
                for j in range(TG):
                    t = TG * i + j
                    wait(dve, "sg_turned", t + 1)
                    nc.vector.tensor_tensor(tile_of(xtok, t), tile_of(xtok, t), bank[j % 2][:, 0:D], ALU.add).then_inc(S["sg_add"], 1)

            steps(dve, NG, gnn_add)
            dve.wait_ge(S["sg_add"], NT)
            row_stats(xtok)
            dve.wait_ge(S["sd_made"], 2)
            link(nc.vector.reciprocal(rstd[:, :], rstd[:, :]))

            def normed(i, j, s, slot_free):
                t = TG * i + j
                wait(dve, s, slot_free)
                return nc.vector.tensor_scalar(ytok[:, j, :], tile_of(xtok, t), mv[:, bass.ds(t, 1), 0],
                                               rstd[:, bass.ds(t, 1)], ALU.subtract, ALU.mult)

            def y_rows(i):
                for j in range(TG):
                    wait(dve, "y_stats", TG * i + j + 1 - TG)
                    normed(i, j, "y_turned", TG * i + j + 1 - TG).then_inc(S["y_made"], 1)
                for j in range(TG):
                    t = TG * i + j
                    wait(dve, "y_made", t + 1)
                    nc.vector.bn_stats(tile_of(stats, t), ytok[:, j, :]).then_inc(S["y_stats"], 1)

            steps(dve, NG, y_rows)
            fence()
            for t in range(NT):
                nc.vector.bn_aggr(mv2[:, t, :], stats[:, t, :])
            fence()
            nc.vector.tensor_scalar(mv2[:, :, 1], mv2[:, :, 1], EPS, None, ALU.add).then_inc(S["var_made"], 1)
            dve.wait_ge(S["sd_made"], 3)
            link(nc.vector.reciprocal(rstd2[:, :], rstd2[:, :]))
            dve.wait_ge(S["y_turned"], NT)

            dve.wait_ge(S["y_stats"], NT)
            dve.wait_ge(S["sg_turned"], NT)

            def xn2_rows(i):
                for j in range(TG):
                    wait(dve, "xn2_made", TG * i + j + 1 - TG)
                    normed(i, j, "y_turned", 0).then_inc(S["y_made"], 1)
                for j in range(TG):
                    t = TG * i + j
                    wait(dve, "y_made", NT + t + 1)
                    nc.vector.tensor_scalar(tile_of(xrow, t), ytok[:, j, :], mv2[:, bass.ds(t, 1), 0],
                                            rstd2[:, bass.ds(t, 1)], ALU.subtract, ALU.mult).then_inc(S["xn2_made"], 1)

            steps(dve, NG, xn2_rows)
            bc = lambda a: a.unsqueeze(2).to_broadcast([P, NT, EXP])
            dve.wait_ge(S["router_mm"], NT)
            link(nc.vector.tensor_copy(lg, bank[5][:, 0:NT * EXP].rearrange("p (t e) -> p t e", t=NT)))
            link(nc.vector.tensor_reduce(out=rmax, in_=lg, op=ALU.max, axis=AXX))
            nc.vector.tensor_tensor(lg, lg, bc(rmax), ALU.subtract).then_inc(S["router_in"], 1)
            dve.wait_ge(S["router_exp"], 1)
            link(nc.vector.tensor_reduce(out=rsum, in_=pr, op=ALU.add, axis=AXX))
            link(nc.vector.reciprocal(rrec, rsum))
            link(nc.vector.tensor_tensor(pr, pr, bc(rrec), ALU.mult))
            for t in range(NT):
                last = nc.vector.max(top[:, t, :], pr[:, t, :])
            link(last)
            for t in range(NT):
                last = nc.vector.max_index(topi[:, t, :], top[:, t, :], pr[:, t, :])
            link(last)
            link(nc.vector.tensor_copy(topf, topi))
            link(nc.vector.tensor_tensor(rsum, top[:, :, 0], top[:, :, 1], ALU.add))
            link(nc.vector.reciprocal(rrec, rsum))
            link(nc.vector.tensor_tensor(top[:, :, 0:2], top[:, :, 0:2], rrec.unsqueeze(2).to_broadcast([P, NT, 2]), ALU.mult))
            eid = iota_w[:, 0:EXP].unsqueeze(1).to_broadcast([P, NT, EXP])
            real = bc(node_in[:, :])
            for c in range(TOPK):
                link(nc.vector.tensor_tensor(hit[c], eid, bc(topf[:, :, c]), ALU.is_equal))
            link(nc.vector.tensor_tensor(chosen, hit[0], hit[1], ALU.add))
            nc.vector.tensor_tensor(chosen, chosen, real, ALU.mult).then_inc(S["sel_made"], 1)
            dve.wait_ge(S["sel_mm"], 2)
            link(nc.vector.tensor_copy(before, bank[6][:, 0:NT * EXP].rearrange("p (t e) -> p t e", t=NT)))
            link(nc.vector.tensor_copy(tile_cnt, bank[7][:, 0:NT * EXP].rearrange("p (t e) -> p e t", t=NT)))
            for e in range(EXP):
                last = nc.vector.tensor_tensor_scan(upto[:, e, :], ones[:, 0:NT], tile_cnt[:, e, :], 0.0, ALU.mult, ALU.add)
            link(last)
            link(nc.vector.tensor_scalar(cnt_i, upto[:, :, NT - 1], float(P - 1), None, ALU.add))
            link(nc.vector.tensor_scalar(cnt_i, cnt_i, 7, None, ALU.arith_shift_right))
            link(nc.vector.tensor_copy(ntl, cnt_i))
            link(nc.vector.tensor_tensor_scan(tend, ones[:, 0:EXP], ntl, 0.0, ALU.mult, ALU.add))
            link(nc.vector.tensor_tensor(sbase, tend, ntl, ALU.subtract))
            link(nc.vector.tensor_scalar(sbase, sbase, float(P), None, ALU.mult))
            link(nc.vector.tensor_tensor(upto, upto, tile_cnt, ALU.subtract))
            link(nc.vector.tensor_tensor(upto, upto, sbase.unsqueeze(2).to_broadcast([P, EXP, NT]), ALU.add))
            link(nc.vector.tensor_tensor(before, before, upto.rearrange("p e t -> p t e"), ALU.add))
            for c in range(TOPK):
                link(nc.vector.tensor_tensor(lg, hit[c], before, ALU.mult))
                link(nc.vector.tensor_reduce(out=spos, in_=lg, op=ALU.add, axis=AXX))
                link(nc.vector.tensor_tensor(spos, spos, node_in[:, :], ALU.mult))
                ins = nc.vector.tensor_tensor(pos[:, c, :], spos, pad_pos[:, c, :], ALU.add)
                link(ins) if c == 0 else ins.then_inc(S["slots_made"], 1)
            link(nc.vector.tensor_tensor(past, iota_w[:, 0:XS_T].unsqueeze(2).to_broadcast([P, XS_T, EXP]),
                                         tend.unsqueeze(1).to_broadcast([P, XS_T, EXP]), ALU.is_ge))
            link(nc.vector.tensor_reduce(out=slot_expf, in_=past, op=ALU.add, axis=AXX))
            nc.vector.tensor_scalar(slot_exp, slot_expf, float(EXP - 1), None, ALU.min).then_inc(S["slots_made"], 1)
            dve.wait_ge(S["b1_mm"], 1)
            for h in range(2):
                nc.vector.tensor_copy(xnt_b1[0:EXP, h * 512:(h + 1) * 512], bank[3 + h][0:EXP, :]).then_inc(S["b1_out"], 1)
            for e in range(EXP):
                nc.vector.tensor_scalar(w1a[:, 0, e * HF:(e + 1) * HF], w1a[:, 0, e * HF:(e + 1) * HF], gcols[:, e, 0:1], None,
                                        ALU.mult).then_inc(S["w_scaled"], 1)

            def slot(i):
                for c in range(2):
                    s = 2 * i + c
                    wait(dve, "hid_turned", 2 * s)
                    dve.wait_ge(s_bias[c], i * 32 + 32)
                    for h in range(2):
                        dve.wait_ge(S["hid_mm"], 2 * s + h + 1)
                        nc.vector.tensor_tensor(hrow[:, h * 512:(h + 1) * 512], bank[1 + h][:, :], b1t[c][:, h * 512:(h + 1) * 512],
                                                ALU.add).then_inc(S["hid_pre"], 1)
                    dve.wait_ge(S["hid_turned"], 2 * s + 1)
                    nc.vector.tensor_copy(hTq[:, 0:HC // 2, :], bank[3][:, :].rearrange("p (q n) -> p q n", q=HC // 2)).then_inc(S["hid_back_v"], 1)
                    dve.wait_ge(S["out_mm"], s + 1)
                    wait(dve, s_ys[c], i * 16)
                    nc.vector.tensor_tensor(orow[c], bank[5 + c][:, 0:D], b2t[c], ALU.add).then_inc(S["out_back"], 1)

            dve.wait_ge(S["scat_st"], 16 * TOPK * NT)
            slot(0)
            with dve.Fori(1, SLOT_T // 2) as i:
                slot(i)
            for g in range(NG):
                for c in range(TOPK):
                    b = (2 * g + c) % 4
                    dve.wait_ge(s_back[b], 16 * TG * ((2 * g + c) // 4 + 1))
                    if c:
                        dve.wait_ge(S["combined"], TG * (2 * g + 1))
                    for j in range(TG):
                        t = g * TG + j
                        nc.vector.scalar_tensor_tensor(out=xtok[:, t, :], in0=back[b][:, j, :], scalar=top[:, t, c:c + 1],
                                                       in1=xtok[:, t, :], op0=ALU.mult, op1=ALU.add).then_inc(S["combined"], 1)

        @block.tensor
        def _(pe):
            pe.wait_ge(S["const"], 8)
            pe.wait_ge(S["edges_made"], 2)
            for b, (a, n0, n1) in enumerate(((e_idx, 0, 4), (e_idx, 4, EC), (e_loc, 0, 4), (e_loc, 4, EC), (e_dstf, 0, 4), (e_dstf, 4, EC))):
                for c in range(n0, n1):
                    m = nc.tensor.transpose(bank[b][:, (c - n0) * P:(c - n0 + 1) * P], a[:, c, :], ident[:, :])
                m.then_inc(S["edge_turned"], 1)
            pe.wait_ge(S["edges_made"], 3)
            nc.tensor.matmul(bank[6][:, 0:1], ones[:, :], e_viol, start=True, stop=True).then_inc(S["viol_sum"], 1)
            pe.wait_ge(S["edge_back"], 6)
            pe.wait_ge(S["flag_set"], 1)

            for l in range(LAYERS):
                pe.wait_ge(S["wrel_in"], 48 * (l + 1))
                if l == 0:
                    pe.wait_ge(S["mixw_in"], 48)
                    pe.wait_ge(S["win_out"], 16)

                def node(i):
                    if l == 0:
                        for j in range(TG):
                            t = TG * i + j
                            wait(pe, "xn_made", t + 1)
                            wait(pe, "stage_full", t if j == 0 else t - 1)
                            for k in range(KD):
                                m = nc.tensor.transpose(bank[6 + j % 2][:, k * P:(k + 1) * P], xnt[:, j, k * P:(k + 1) * P], ident[:, :])
                            m.then_inc(S["xn_turned"], 1)
                    for j in range(TG):
                        t = TG * i + j
                        wait(pe, "stage_full", NT * l + t + 1)
                        for c in range(4):
                            wait(pe, "y_act" if c % 2 == 0 else "y_dve", 2 * NT * l + 2 * t + c // 2 - 1)
                            for k in range(KD):
                                m = nc.tensor.matmul(bank[c][:, :], stage[:, j, k, :], wrel[:, k, c * 512:(c + 1) * 512],
                                                     start=k == 0, stop=k == KD - 1)
                            m.then_inc(S["y_mm"], 1)
                        wait(pe, "root_out", KD * (NT * l + t))
                        if l == 0:
                            wait(pe, "qkv_out", t)
                            for o in range(3):
                                for k in range(KD):
                                    w = wqkv_sb[:, k, o * P:(o + 1) * P]
                                    h = stage[:, j, k, :]
                                    nc.tensor.matmul(bank[5][:, o * P:(o + 1) * P], h if o == 2 else w, w if o == 2 else h,
                                                     start=k == 0, stop=k == KD - 1)
                        for e in range(KD):
                            for k in range(KD):
                                m = nc.tensor.matmul(bank[4][:, e * P:(e + 1) * P], wroot[:, k, e * P:(e + 1) * P], stage[:, j, k, :],
                                                     start=k == 0, stop=k == KD - 1)
                        m.then_inc(S["node_mm"], 1)

                steps(pe, NG, node)
                if l == 0:
                    pe.wait_ge(S["kexp_made"], 1)
                    for t in range(NT + 1):
                        if t < NT:
                            rows = P if t < NT - 1 else LAST
                            if t >= 2:
                                pe.wait_ge(S["k_out"], t - 1)
                            nc.tensor.transpose(bank[t % 2][0:rows, 0:P], kT[:, t * P:t * P + rows], ident[:, :]).then_inc(S["k_turned"], 1)
                        if t >= 1:
                            rows = P if t < NT else LAST
                            pe.wait_ge(S["k_out"], t)
                            nc.tensor.matmul(bank[2][:, 0:P], vtok[0:rows, t - 1, :], ktok[0:rows, (t - 1) % 2, :],
                                             start=t == 1, stop=t == NT).then_inc(S["ctx_mm"], 1)
                    pe.wait_ge(S["ctx_out"], 1)
                    nc.tensor.matmul(bank[3][:, 0:D], ctxT, wout_sb, start=True, stop=True).then_inc(S["mctx_mm"], 1)
                    pe.wait_ge(S["mctx_out"], 1)
                    pe.wait_ge(S["root_out"], KD * NT)
                    for t in range(NT):
                        if t >= 4:
                            pe.wait_ge(S["mix_add"], t - 3)
                        nc.tensor.matmul(bank[4 + t % 4][:, 0:D], qT[:, t * P:(t + 1) * P], mctx, start=True, stop=False)
                        nc.tensor.matmul(bank[4 + t % 4][:, 0:D], ones[0:1, :], bout_sb[0:1, :], start=False, stop=True).then_inc(S["mix_mm"], 1)
                pe.wait_ge(S["y_act"], 2 * NT * (l + 1))
                pe.wait_ge(S["y_dve"], 2 * NT * (l + 1))
                outside = pe.value_load(flag[0:1, 0:1], min_val=0, max_val=1)
                with pe.If(outside < 1):
                    def tiles(i):
                        for j in range(STEP):
                            n = ETILES * l + STEP * i + j
                            if j % HALF == 0:
                                wait(pe, "hot_ready", 2 * (STEPS + 1) * l + 2 * i + j // HALF + 1)
                            wait(pe, s_gath[j], 16 * (STEPS * l + i + 1))
                            wait(pe, "tile_add", n - 1)
                            for k in range(KD):
                                m = nc.tensor.matmul(bank[j % 2][:, k * WIN:(k + 1) * WIN], gath[:, j, k * P:(k + 1) * P],
                                                     onehot[:, j, :], start=True, stop=True)
                            m.then_inc(S["tile_mm"], 1)

                    steps(pe, STEPS, tiles)
                with pe.Else():
                    with pe.Fori(0, STEPS) as i:
                        for j in range(STEP):
                            n = ETILES * l + i * STEP + j
                            pe.wait_ge(s_gath[j], (i + (STEPS * l + 1)) * 16)
                            pe.nop(nofuse=True)
                            with pe.Fori(0, NGW) as v:
                                pe.wait_ge(S["gen_hot"], n * (2 * NGW + 1) + v * 2 + 2)
                                for k in range(KD):
                                    m = nc.tensor.matmul(bank[k][:, 0:GWIN], gath[:, j, k * P:(k + 1) * P], ghot,
                                                         start=True, stop=True)
                                m.then_inc(S["gen_mm"], 1)
                            pe.wait_ge(S["gen_add"], (n + 1) * NGW * KD)
                            pe.nop(nofuse=True).then_inc(S["tile_mm"], 1)

            pe.wait_ge(S["layer_done"], LAYERS)

            def gnn_turn(i):
                for j in range(TG):
                    t = TG * i + j
                    wait(pe, "sg_made", t + 1)
                    wait(pe, "sg_add", t if j == 0 else t - 1)
                    for k in range(KD):
                        m = nc.tensor.transpose(bank[j % 2][:, k * P:(k + 1) * P], yT[:, j, k, :], ident[:, :])
                    m.then_inc(S["sg_turned"], 1)

            steps(pe, NG, gnn_turn)
            pe.wait_ge(S["sg_add"], NT)
            pe.wait_ge(S["ffw_in"], 16 * FFW)

            def router(i):
                for j in range(TG):
                    t = TG * i + j
                    wait(pe, "y_made", t + 1)
                    wait(pe, "y_out", t if j == 0 else t - 1)
                    for k in range(KD):
                        m = nc.tensor.transpose(bank[j % 2][:, k * P:(k + 1) * P], ytok[:, j, k * P:(k + 1) * P], ident[:, :])
                    m.then_inc(S["y_turned"], 1)
                for j in range(TG):
                    t = TG * i + j
                    wait(pe, "y_out", t + 1)
                    o = bank[5][:, bass.ds(t * EXP, EXP)]
                    for k in range(KD):
                        nc.tensor.matmul(o, yT[:, j, k, :], wr_sb[:, k, :], start=k == 0, stop=False)
                    nc.tensor.matmul(o, ones[0:1, :], br_sb[0:1, :], start=False, stop=True).then_inc(S["router_mm"], 1)

            steps(pe, NG, router)
            pe.wait_ge(s_wexp[0], 16 * KD)
            pe.wait_ge(S["bsel_made"], 1)
            for h in range(2):
                for e in range(EXP):
                    for k in range(KD):
                        nc.tensor.matmul(bank[3 + h][0:EXP, :], bsel[:, e, k, :], w1a[:, k, e * HF + h * 512:e * HF + (h + 1) * 512],
                                         start=e == 0 and k == 0, stop=False)
                m = nc.tensor.matmul(bank[3 + h][0:EXP, :], ident[0:EXP, 0:EXP], b1_sb[0:EXP, h * 512:(h + 1) * 512],
                                     start=False, stop=True)
            m.then_inc(S["b1_mm"], 1)
            pe.wait_ge(S["sel_made"], 1)
            flat = chosen.rearrange("p t e -> p (t e)")
            nc.tensor.matmul(bank[6][:, 0:NT * EXP], tri[:, :], flat, start=True, stop=True).then_inc(S["sel_mm"], 1)
            nc.tensor.matmul(bank[7][:, 0:NT * EXP], ones[:, :], flat, start=True, stop=True).then_inc(S["sel_mm"], 1)

            def turn_rows(s, c):
                wait(pe, "xs_back", s)
                pe.wait_ge(s_xs[c], 16 * (s // 2 + 1) if isinstance(s, int) else 0)
                for k in range(KD):
                    m = nc.tensor.transpose(bank[0][:, k * P:(k + 1) * P], xs[c][:, k * P:(k + 1) * P], ident[:, :])
                m.then_inc(S["xs_turned"], 1)

            def hidden(s, c):
                e = pe.value_load(slot_exp[0:1, bass.ds(s, 1)], min_val=0, max_val=EXP - 1)
                pe.wait_ge(S["xs_back"], s + 1)
                for h in range(2):
                    wait(pe, "hid_pre", 2 * s + h - 1)
                    for k in range(KD):
                        m = nc.tensor.matmul(bank[1 + h][:, :], xsT[c][:, k, :], w1a[:, k, bass.ds(e * HF + h * 512, 512)],
                                             start=k == 0, stop=k == KD - 1)
                    m.then_inc(S["hid_mm"], 1)

            def slot(i):
                for c in range(2):
                    s = 2 * i + c
                    for h in range(2):
                        pe.wait_ge(S["hid_act"], 2 * s + h + 1)
                        wait(pe, "hid_back_s" if h else "hid_back_v", s)
                        for q in range(HC // 2):
                            m = nc.tensor.transpose(bank[3 + h][:, q * P:(q + 1) * P], hrow[:, h * 512 + q * P:h * 512 + (q + 1) * P], ident[:, :])
                        m.then_inc(S["hid_turned"], 1)
                    hidden(s + 1, 1 - c)
                    pe.wait_ge(S["xs_back"], s + 2)
                    pe.wait_ge(s_xs[c], i * 16 + 32)
                    for k in range(KD):
                        m = nc.tensor.transpose(bank[0][:, k * P:(k + 1) * P], xs[c][:, k * P:(k + 1) * P], ident[:, :])
                    m.then_inc(S["xs_turned"], 1)
                    e = pe.value_load(slot_exp[0:1, bass.ds(s, 1)], min_val=0, max_val=EXP - 1)
                    pe.wait_ge(S["hid_back_v"], s + 1)
                    pe.wait_ge(S["hid_back_s"], s + 1)
                    wait(pe, "out_back", s - 1)
                    for q in range(HC):
                        m = nc.tensor.matmul(bank[5 + c][:, 0:D], hTq[:, q, :], w2a[:, q, bass.ds(e * D, D)],
                                             start=q == 0, stop=q == HC - 1)
                    m.then_inc(S["out_mm"], 1)

            pe.wait_ge(S["slots_made"], 2)
            pe.wait_ge(S["w_scaled"], 2 * EXP)
            pe.wait_ge(S["b1_out"], 2)
            pe.wait_ge(s_wexp[1], 16 * HC)
            turn_rows(0, 0)
            turn_rows(1, 1)
            hidden(0, 0)
            slot(0)
            with pe.Fori(1, SLOT_T // 2) as i:
                slot(i)


_INS = ["x", "src", "dst", "edge_type_8", "L0_gnn_weights", "L0_gnn_roots", "L0_gnn_biases", "L0_mix_W_qkv",
        "L0_mix_W_out", "L0_mix_b_out", "L0_ffn_Wr", "L0_ffn_br", "L0_ffn_ln_g", "L0_ffn_ln_b",
        "L0_ffn_W1", "L0_ffn_b1", "L0_ffn_W2", "L0_ffn_b2"]


def kernel(**inputs):
    import numpy as _np
    import concourse.bacc as _bacc
    from concourse import mybir as _mybir
    from concourse.bass_utils import run_bass_kernel_spmd as _run

    nc = _bacc.Bacc("TRN2", target_bir_lowering=False, num_devices=1)
    arrays, args = {}, []
    for name in _INS:
        a = _np.ascontiguousarray(inputs[name])
        arrays[f"in_{name}_dram"] = a
        args.append(nc.dram_tensor(f"in_{name}_dram", a.shape, _mybir.dt.from_np(a.dtype), kind="ExternalInput").ap())
    args.append(nc.dram_tensor("out_0_dram", (N_NODES, D), _mybir.dt.float32, kind="ExternalOutput").ap())
    gps_layer(nc, *args)
    r = _run(nc, [arrays], core_ids=[0])
    return r.results[0]["out_0_dram"]
```

```python
import concourse.bass as bass
from concourse import mybir
from contextlib import ExitStack

F32 = mybir.dt.float32
I32 = mybir.dt.int32
U32 = mybir.dt.uint32
ALU = mybir.AluOpType
ACT = mybir.ActivationFunctionType
AXX = mybir.AxisListType.X

P = 128
N_NODES, D = 3125, 256
KD = D // P
NT = -(-N_NODES // P)
NP = NT * P
LAST = N_NODES - (NT - 1) * P
TG = 5
NG = NT // TG
REL, LAYERS = 8, 3
EDGES = 103125
WIN = 64
GWIN = 400
NGW = NP // GWIN
ETILES = -(-EDGES // P)
SPAN = 34
SPANS = -(-ETILES // SPAN)
STEP = SPAN // 2
HALVES = (range(0, STEP // 2), range(STEP // 2, STEP))
STEPS = 2 * SPANS
LAST_TILES = ETILES - (STEPS - 1) * STEP
assert 0 < LAST_TILES <= len(HALVES[0])
TURNS = 2 * STEPS - 1
SPAN_INV = -(-(1 << 16) // SPAN)
assert all(n * SPAN_INV >> 16 == n // SPAN for n in range(-(-ETILES // P) * P))
CATCH_UP = 12
BEFORE_LAST = SPANS - 2
INNER_T = SPANS
assert INNER_T == NT - 1
LAST_READY = 13
ALONE = {7: 0, 12: 1, 17: 2, 22: 3, 26: 4}
EARLY = {2: 0, 3: 1, 4: 2, 5: 3, 6: 4}
LATER = {18: 0, 20: 1, 22: 2, 24: 3, 26: 4}
AT_LAST = {LAST_READY + 1: 0, LAST_READY + 2: 1, LAST_READY + 3: 2, LAST_READY + 4: 3, ETILES - (SPANS - 1) * SPAN - 1: 4}
READY = ((ALONE, 0), (EARLY, 0), (LATER, STEP), (AT_LAST, LAST_READY))
MIX_AT = 8
assert MIX_AT + NT < SPAN
MIX_STEPS = {(1, 1): 0, (2, 0): 13}
MIX_END = (13, NT)
BESIDE = dict(rows=1, turn=3, stage=4, qkv=6, qkv_out=9, root=14, add=19)
FIRST = dict(rows=0, turn=1, stage=1, qkv=2, qkv_out=3, root=4, add=5)
SECOND = dict(rows=7, turn=9, stage=9, qkv=11, qkv_out=14, root=17, add=22)
FINAL = dict(rows=0, turn=2, stage=2, qkv=4, qkv_out=6, root=8, add=11)
assert FINAL["add"] < LAST_READY
W1_PACE = 40
EC = -(-ETILES // P)
FULL_C = EDGES // (P * P)
FULL_R = (EDGES - FULL_C * P * P) // P
REST = EDGES - FULL_C * P * P - FULL_R * P
NO_NODE = 8192.0
HEADS, DH = 4, 32
HID = HEADS * DH
EXP, HF = 8, 1024
HC = HF // P
TOK = TG * P
TOPK = 2
SLOT_T = (TOPK * N_NODES + EXP * (P - 1)) // P
SLOT_T += SLOT_T % 2
SLOTS = SLOT_T * P
XS_T = SLOT_T + 3
ZERO_T = XS_T // NT
EPS = 1e-5
ARENA = 38300
FFW = 2 * EXP + 3


def gps_layer(nc, x, src, dst, etype, gw, groots, gbias, wqkv, wout, bout,
              Wr, br, ln_g, ln_b, W1, b1, W2, b2, out):
    ctx = ExitStack()
    with ctx:
        ctx.enter_context(nc.allow_non_contiguous_dma(reason="short bias and window columns"))

        def sb(name, shape, dt=F32):
            return ctx.enter_context(nc.sbuf_tensor(name, shape, dt))

        y_dram = [nc.dram_tensor(f"y_dram{i}", (NP * REL, D), F32).ap() for i in range(2)]
        xs_dram = nc.dram_tensor("xs_dram", (XS_T * P, D), F32).ap()
        ys_dram = nc.dram_tensor("ys_dram", (XS_T * P, D), F32).ap()
        b1_dram = nc.dram_tensor("b1_dram", (EXP, HF), F32).ap()
        win_dram = nc.dram_tensor("win_dram", (EC * P,), I32).ap()

        xtok = sb("xtok", [P, NT, D])
        hT_all = sb("hT_all", [P, NP, KD])
        ident = sb("ident", [P, P])
        ones = sb("ones", [P, P])
        zcol = sb("zcol", [P, 1])
        iota_w = sb("iota_w", [P, GWIN])
        stats = sb("stats", [P, NT, 6])
        mv = sb("mv", [P, NT, 2])
        rstd = sb("rstd", [P, NT])
        mv2 = sb("mv2", [P, NT, 2])
        rstd2 = sb("rstd2", [P, NT])
        zrow = sb("zrow", [P, D])
        tri = sb("tri", [P, P])
        node_in = sb("node_in", [P, NT])
        pad_pos = sb("pad_pos", [P, TOPK, NT])
        pos = sb("pos", [P, TOPK, NT], I32)
        flag = sb("flag", [P, 1], I32)
        arena = sb("arena", [P, ARENA])
        used = [0]

        def carve(n):
            a = arena[:, used[0]:used[0] + n]
            used[0] += n
            assert used[0] <= ARENA, used[0]
            return a

        idx_i = carve(EC * P).bitcast(I32)
        dloc = carve(EC * P)
        dabs = carve(EC * P)
        win_row = carve(EC * P).bitcast(I32)
        bias_g = carve(LAYERS * KD).rearrange("p (l k) -> p l k", l=LAYERS)
        gath = carve(STEP * D).rearrange("p (c n) -> p c n", c=STEP)
        onehot = carve(STEP * WIN).rearrange("p (c n) -> p c n", c=STEP)
        ghot = carve(GWIN)
        gcol = carve(2)
        idx_ring = carve(STEP).bitcast(I32)
        wrel = carve(KD * REL * D).rearrange("p (k n) -> p k n", k=KD)
        wroot = carve(KD * D).rearrange("p (k n) -> p k n", k=KD)
        wroot0 = carve(KD * D).rearrange("p (k n) -> p k n", k=KD)
        ybuf = carve(4 * 512).rearrange("p (c n) -> p c n", c=4)
        stage = carve(TG * KD * P).rearrange("p (c k n) -> p c k n", c=TG, k=KD)
        xnt = carve(TG * D).rearrange("p (c n) -> p c n", c=TG)
        wqkv_sb = carve(KD * 3 * HID).rearrange("p (k n) -> p k n", k=KD)
        wout_sb = carve(D)
        bout_sb = carve(D)
        mark = used[0]
        e_src = carve(EC * P).bitcast(I32).rearrange("p (c n) -> p c n", c=EC)
        e_dst = carve(EC * P).bitcast(I32).rearrange("p (c n) -> p c n", c=EC)
        e_typ = carve(EC * P).bitcast(I32).rearrange("p (c n) -> p c n", c=EC)
        e_dstf = carve(EC * P).rearrange("p (c n) -> p c n", c=EC)
        e_idx = carve(EC * P).rearrange("p (c n) -> p c n", c=EC)
        e_loc = carve(EC * P).rearrange("p (c n) -> p c n", c=EC)
        e_in = carve(EC * P).rearrange("p (c n) -> p c n", c=EC)
        e_win = carve(EC)
        e_wini = carve(EC).bitcast(I32)
        e_viol = carve(2)
        e_late = carve(EC)
        e_span = carve(EC).bitcast(I32)
        e_caught = carve(EC)
        e_final = carve(EC)
        used[0] = mark
        qT = carve(NP)
        kT = carve(NP)
        vtok = carve(NP).rearrange("p (t n) -> p t n", t=NT)
        ktok = carve(2 * P).rearrange("p (c n) -> p c n", c=2)
        nkmax = carve(1)
        ksum = carve(1)
        krec = carve(1)
        ctxT = carve(P)
        mctx = carve(D)
        used[0] = 0
        w2a = carve(EXP * HC * D).rearrange("p (q e n) -> p q (e n)", e=EXP, q=HC)
        w1a = carve(EXP * KD * HF).rearrange("p (k e n) -> p k (e n)", e=EXP, k=KD)
        gcols = carve(EXP * KD).rearrange("p (e k) -> p e k", e=EXP)
        bcols = carve(EXP * KD).rearrange("p (k e) -> p k e", e=EXP)
        bsel = carve(EXP * KD * EXP).rearrange("p (e k f) -> p e k f", e=EXP, k=KD)
        b1_sb = carve(HF)
        wr_sb = carve(KD * EXP).rearrange("p (k n) -> p k n", k=KD)
        br_sb = carve(EXP)
        lg = carve(NT * EXP).rearrange("p (t e) -> p t e", t=NT)
        pr = carve(NT * EXP).rearrange("p (t e) -> p t e", t=NT)
        hit = [carve(NT * EXP).rearrange("p (t e) -> p t e", t=NT) for _ in range(TOPK)]
        chosen = carve(NT * EXP).rearrange("p (t e) -> p t e", t=NT)
        top = carve(NT * 8).rearrange("p (t e) -> p t e", t=NT)
        topi = carve(NT * 8).bitcast(U32).rearrange("p (t e) -> p t e", t=NT)
        topf = pr
        rmax = carve(NT)
        rsum = carve(NT)
        rrec = carve(NT)
        cnt_i = carve(EXP).bitcast(I32)
        ntl = carve(EXP)
        tend = carve(EXP)
        sbase = carve(EXP)
        slot_exp = carve(XS_T).bitcast(I32)
        slot_expf = carve(XS_T)
        spos = carve(NT)
        ytok = carve(TG * D).rearrange("p (c n) -> p c n", c=TG)
        yT = carve(TG * KD * P).rearrange("p (c k n) -> p c k n", c=TG, k=KD)
        used[0] -= TG * KD * P
        before = carve(NT * EXP).rearrange("p (t e) -> p t e", t=NT)
        tile_cnt = carve(EXP * NT).rearrange("p (e t) -> p e t", t=NT)
        upto = carve(EXP * NT).rearrange("p (e t) -> p e t", t=NT)
        past = carve(XS_T * EXP).rearrange("p (s e) -> p s e", s=XS_T)
        sgT, turned_y, yrow = yT[:, 0, :, :], yT[:, 1, :, :], ytok[:, 0, :]
        hflat = hT_all[:, :, :].rearrange("p n k -> p (n k)")
        hrow = hflat[:, 0:HF]
        hTq = hflat[:, HF:2 * HF].rearrange("p (q n) -> p q n", q=HC)
        b1t = [hflat[:, (2 + i) * HF:(3 + i) * HF] for i in range(2)]
        b2t = [hflat[:, 4 * HF + i * D:4 * HF + (i + 1) * D] for i in range(2)]
        xs = [ytok[:, i, :] for i in range(2)]
        orow = [ytok[:, 2 + i, :] for i in range(2)]
        xsT = [yT[:, i, :, :] for i in range(2)]
        back = [w2a[:, q, 0:TG * D].rearrange("p (j d) -> p j d", j=TG) for q in range(4)]

        bank = [ctx.enter_context(nc.psum_tensor(f"bank{i}", [P, 512], F32)) for i in range(8)]

        names = """edge_in gb_in wrel_in mixw_in ffw_in win_out win_in out_st
            const pads edges_made edge_turned edge_back viol_sum flag_set node_ready
            var_made sd_made xn_made xn_turned stage_full
            y_mm y_act y_dve node_mm root_out qkv_out
            late_made late_turned late_staged qkv_mm late_mm late_added
            ix_ready tile_mm hot_ready tile_add gen_hot gen_mm gen_add layer_done
            x_biased kmax_made kexp_made k_turned k_out ctx_mm ctx_out mctx_mm mctx_out mix_mm mix_add
            sg_made sg_turned sg_add x2_var x2_sd norm_step y_made y_turned y_out xn2_made
            router_mm router_in router_exp bsel_made b1_mm b1_added b1_st sel_made sel_mm slots_made w_scaled zero_st
            scat_st xs_turned xs_back hid_mm hid_pre hid_act hid_turned hid_back_v hid_back_s out_mm out_back
            combined chain_v""".split()
        S = {n: ctx.enter_context(nc.semaphore(n)) for n in names}
        s_gath = [ctx.enter_context(nc.semaphore(f"gath{j}")) for j in range(STEP)]
        s_x = [ctx.enter_context(nc.semaphore(f"x_in{g}")) for g in range(NG)]
        s_yst = [ctx.enter_context(nc.semaphore(f"y_stored{c}")) for c in range(4)]
        s_wexp = [ctx.enter_context(nc.semaphore(f"w{c}_in")) for c in (1, 2)]
        s_xs = [ctx.enter_context(nc.semaphore(f"xs_in{c}")) for c in range(2)]
        s_bias = [ctx.enter_context(nc.semaphore(f"bias_in{c}")) for c in range(2)]
        s_ys = [ctx.enter_context(nc.semaphore(f"ys_out{c}")) for c in range(2)]
        s_back = [ctx.enter_context(nc.semaphore(f"back_in{c}")) for c in range(4)]
        block = ctx.enter_context(nc.Block())

        def wait(eng, s, v):
            if isinstance(v, int) and v <= 0:
                return
            eng.wait_ge(S[s] if isinstance(s, str) else s, v)

        def wait_apart(eng, s, v):
            wait(eng, s, v)
            eng.nop(nofuse=True)

        def steps(eng, n, body):
            body(0)
            with eng.Fori(1, n) as i:
                body(i)

        def edge_loop(span, eng):
            span(0, ())
            span(1, ())
            span(2, ((0, ALONE),))
            with eng.Fori(3, CATCH_UP) as m:
                span(m, ((m - 2, ALONE),))
            span(CATCH_UP, ((CATCH_UP - 2, EARLY), (CATCH_UP - 1, LATER)))
            with eng.Fori(CATCH_UP + 1, BEFORE_LAST) as m:
                span(m, ((m - 1, ALONE),))
            span(BEFORE_LAST, ((BEFORE_LAST - 1, EARLY), (BEFORE_LAST, LATER)))
            span(SPANS - 1, ((SPANS - 1, AT_LAST),))

        def ready_at(at):
            return [u for a, u in READY if a is at][0]

        def is_step(l, m, layer, step):
            return l == layer and isinstance(m, int) and m == step

        def mix_tile(l, m, u):
            first = MIX_STEPS.get((l, m)) if isinstance(m, int) else None
            if first is None or u % 2 == 0 or first + u // 2 >= min(e for e in MIX_END if e > first):
                return None
            return first + u // 2

        def beside(l, m, u, part):
            if l > 0:
                return []
            if is_last(m):
                tiles = ((NT - 1, FINAL),)
            elif isinstance(m, int) and m == 0:
                tiles = ((0, FIRST), (1, SECOND))
            else:
                tiles = ((m + 1, BESIDE),)
            return [t for t, at in tiles if at[part] == u]

        def is_last(m):
            return isinstance(m, int) and m == SPANS - 1

        def gathered(l, i, j):
            return (i + (STEPS - (j >= LAST_TILES)) * l + 1) * 16

        def features(t):
            return hT_all[:, bass.ds(t * P, P), :].rearrange("p n k -> p k n")

        def expert_rows(t):
            return hT_all[:, bass.ds(t * P, P), :].rearrange("p n k -> p (n k)")

        def groups(eng, ahead, work, ahead_first=False):
            for j in range(TG):
                ahead(0, j)

            def group(i, more):
                for j in range(TG):
                    if more and ahead_first:
                        ahead(i + 1, j)
                    work(i, j)
                    if more and not ahead_first:
                        ahead(i + 1, j)

            group(0, True)
            with eng.Fori(1, NG - 1) as i:
                group(i, True)
            group(NG - 1, False)

        def tile_of(a, t):
            return a[:, bass.ds(t, 1), :].rearrange("p o n -> p (o n)")

        w_rel = gw.rearrange("l r (k p) n -> l p k r n", p=P)
        w_root = groots.rearrange("l (k p) n -> l p k n", p=P)

        @block.sync
        def _(sp):
            sp.wait_ge(S["pads"], 4)
            at0, at1 = FULL_C * P * P, FULL_C * P * P + FULL_R * P
            for a, e in ((src, e_src), (dst, e_dst), (etype, e_typ)):
                sp.dma_start(e[:, 0:FULL_C, :], a[0:at0].rearrange("(c p l) -> p c l", p=P, l=P)).then_inc(S["edge_in"], 16)
                sp.dma_start(e[0:FULL_R, FULL_C, :], a[at0:at1].rearrange("(p l) -> p l", l=P)).then_inc(S["edge_in"], 16)
                sp.dma_start(e[FULL_R:FULL_R + 1, FULL_C, 0:REST], a[at1:EDGES].rearrange("(p l) -> p l", p=1)).then_inc(S["edge_in"], 16)
            for g in range(NG):
                full = min(TG * (g + 1), NT - 1)
                sp.dma_start(xtok[:, TG * g:full, :], x[TG * g * P:full * P, :].rearrange("(t p) d -> p t d", p=P)).then_inc(s_x[g], 16)
            sp.dma_start(xtok[0:LAST, NT - 1, :], x[(NT - 1) * P:N_NODES, :]).then_inc(s_x[NG - 1], 16)

            def layer_weights(l):
                for k in range(KD):
                    sp.dma_start(wrel[:, k, :].rearrange("p (r n) -> p r n", r=REL), w_rel[l][:, k]).then_inc(S["wrel_in"], 16)
                sp.dma_start(wroot if l else wroot0, w_root[l]).then_inc(S["wrel_in"], 16)

            layer_weights(0)
            sp.dma_start(wqkv_sb, wqkv.rearrange("(k p) n -> p k n", p=P)).then_inc(S["mixw_in"], 16)
            sp.dma_start(wout_sb, wout).then_inc(S["mixw_in"], 16)
            sp.dma_start(bout_sb, bout.rearrange("(o n) -> o n", o=1).to_broadcast([P, D])).then_inc(S["mixw_in"], 16)
            for l in range(LAYERS):
                sp.dma_start(bias_g[:, l, :], gbias[l].rearrange("(k p) -> p k", p=P)).then_inc(S["gb_in"], 16)
            for e in range(EXP):
                sp.dma_start(gcols[:, e, :], ln_g[e].rearrange("(k p) -> p k", p=P)).then_inc(S["ffw_in"], 16)
                sp.dma_start(bcols[:, :, e], ln_b[e].rearrange("(k p) -> p k", p=P)).then_inc(S["ffw_in"], 16)
            sp.dma_start(wr_sb, Wr.rearrange("(k p) n -> p k n", p=P)).then_inc(S["ffw_in"], 16)
            sp.dma_start(br_sb[0:1, :], br.rearrange("(o n) -> o n", o=1)).then_inc(S["ffw_in"], 16)
            sp.dma_start(b1_sb[0:EXP, :], b1).then_inc(S["ffw_in"], 16)
            sp.wait_ge(S["edges_made"], 1)
            sp.dma_start(win_dram.rearrange("(c p) -> p c", p=P), e_wini).then_inc(S["win_out"], 16)
            sp.wait_ge(S["win_out"], 16)
            sp.dma_start(win_row[0:1, :], win_dram.rearrange("(o n) -> o n", o=1)).then_inc(S["win_in"], 16)

            xs_tiles = xs_dram.rearrange("(t p) d -> p t d", p=P)
            sp.wait_ge(S["const"], 9)

            def zeros(n):
                return zrow[:, :].unsqueeze(1).to_broadcast([P, n, D])

            for l in range(LAYERS):
                yd = y_dram[l % 2].rearrange("(t p r) d -> p t (r d)", p=P, r=REL)

                def store(t):
                    for c in range(4):
                        wait(sp, "y_act" if c % 2 == 0 else "y_dve", 2 * NT * l + 2 * t + c // 2 + 1)
                        sp.dma_start(yd[:, bass.ds(t, 1), c * 512:(c + 1) * 512].rearrange("p o n -> p (o n)"),
                                     ybuf[:, c, :]).then_inc(s_yst[c], 16)

                    if l == 0:
                        sp.dma_start(xs_tiles[:, bass.ds(t * ZERO_T, ZERO_T), :], zeros(ZERO_T)).then_inc(S["zero_st"], 16)

                steps(sp, NT, store)
                if l == 0:
                    sp.dma_start(xs_tiles[:, NT * ZERO_T:XS_T, :], zeros(XS_T - NT * ZERO_T)).then_inc(S["zero_st"], 16)
                    sp.dma_start(ys_dram[SLOTS:XS_T * P, :].rearrange("(t p) d -> p t d", p=P), zeros(XS_T - SLOT_T)).then_inc(S["zero_st"], 16)
                if l + 1 < LAYERS:
                    if l == 0:
                        sp.wait_ge(S["y_mm"], 4 * NT)
                    else:
                        sp.wait_ge(S["node_mm"], NT * l)
                    layer_weights(l + 1)
            for c in range(4):
                sp.wait_ge(s_yst[c], 16 * NT * LAYERS)

            sp.wait_ge(S["mix_add"], NT)
            sp.wait_ge(S["node_mm"], NT * (LAYERS - 1))
            for k in range(KD):
                for e in range(EXP):
                    sp.wait_ge(S["tile_mm"], ETILES * (LAYERS - 1) + SPAN + W1_PACE * (k * EXP + e))
                    sp.dma_start(w1a[:, k, e * HF:(e + 1) * HF], W1[e, k * P:(k + 1) * P, :]).then_inc(s_wexp[0], 16)
            sp.wait_ge(S["layer_done"], LAYERS)
            for q in range(HC):
                sp.dma_start(w2a[:, q, :].rearrange("p (e n) -> p e n", e=EXP),
                             W2.rearrange("e (q p) n -> q p e n", p=P)[q]).then_inc(s_wexp[1], 16)
            sp.wait_ge(S["b1_added"], 2)
            sp.dma_start(b1_dram, b1_sb[0:EXP, :]).then_inc(S["b1_st"], 16)
            sp.wait_ge(S["b1_st"], 16)
            sp.wait_ge(S["slots_made"], 2)
            sp.wait_ge(S["scat_st"], 16 * TOPK * NT)

            def load_rows(s, c):
                sp.dma_start(xs[c], xs_dram.rearrange("(t p) d -> p t d", p=P)[:, bass.ds(s, 1), :].rearrange("p o d -> p (o d)")).then_inc(s_xs[c], 16)

            def load_bias(s, c):
                e = sp.value_load(slot_exp[0:1, bass.ds(s, 1)], min_val=0, max_val=EXP - 1)
                sp.dma_start(b1t[c], b1_dram[bass.ds(e, 1), :].to_broadcast([P, HF])).then_inc(s_bias[c], 16)
                sp.dma_start(b2t[c], b2[bass.ds(e, 1), :].to_broadcast([P, D])).then_inc(s_bias[c], 16)

            for c in range(2):
                load_rows(c, c)
                load_bias(c, c)
            sp.wait_ge(S["xs_turned"], 1)
            load_rows(2, 0)

            def feed(i):
                for c in range(2):
                    s = 2 * i + c
                    sp.wait_ge(S["xs_turned"], s + 2)
                    load_rows(s + 3, 1 - c)
                    sp.wait_ge(S["out_back"], s + 1)
                    sp.dma_start(ys_dram[0:SLOTS, :].rearrange("(t p) d -> p t d", p=P)[:, bass.ds(s, 1), :].rearrange("p o d -> p (o d)"), orow[c]).then_inc(s_ys[c], 16)
                    load_bias(s + 2, c)

            feed(0)
            with sp.Fori(1, SLOT_T // 2) as i:
                feed(i)
            for c in range(2):
                sp.wait_ge(s_ys[c], 16 * (SLOT_T // 2))
                sp.wait_ge(s_xs[c], 16 * (SLOT_T // 2 + 2 - c))
                sp.wait_ge(s_bias[c], 32 * (SLOT_T // 2 + 1))
            for g in range(NG):
                sp.wait_ge(S["combined"], TOPK * TG * (g + 1))
                if g < NG - 1:
                    sp.dma_start(out[g * TOK:(g + 1) * TOK, :].rearrange("(t p) d -> p t d", p=P), xtok[:, g * TG:(g + 1) * TG, :]).then_inc(S["out_st"], 16)
                else:
                    sp.dma_start(out[g * TOK:(NT - 1) * P, :].rearrange("(t p) d -> p t d", p=P), xtok[:, g * TG:NT - 1, :]).then_inc(S["out_st"], 16)
                    sp.dma_start(out[(NT - 1) * P:N_NODES, :], xtok[0:LAST, NT - 1, :]).then_inc(S["out_st"], 16)
            sp.wait_ge(S["out_st"], 16 * (NG + 1))

        @block.gpsimd
        def _(pool):
            nc.gpsimd.memset(xtok[:, NT - 1, :], 0.0).then_inc(S["pads"], 1)
            nc.gpsimd.memset(e_src, 0).then_inc(S["pads"], 1)
            nc.gpsimd.memset(e_typ, 0).then_inc(S["pads"], 1)
            nc.gpsimd.memset(e_dst, int(NO_NODE)).then_inc(S["pads"], 1)
            nc.gpsimd.memset(ones[:, :], 1.0).then_inc(S["const"], 1)
            nc.gpsimd.iota(iota_w[:, :], [[1, GWIN]], base=0, channel_multiplier=0,
                           allow_small_or_imprecise_dtypes=True).then_inc(S["const"], 1)
            nc.gpsimd.memset(zrow[:, :], 0.0).then_inc(S["const"], 1)
            nc.gpsimd.memset(tri[:, :], 1.0).then_inc(S["const"], 1)
            nc.gpsimd.iota(pad_pos[:, 0, :], [[P, NT]], base=0, channel_multiplier=1,
                           allow_small_or_imprecise_dtypes=True).then_inc(S["const"], 1)
            nc.gpsimd.iota(e_span, [[P, EC]], base=0, channel_multiplier=1).then_inc(S["const"], 1)
            nc.gpsimd.memset(ident[:, :], 0.0).then_inc(S["const"], 1)
            pool.wait_ge(S["const"], 7)
            nc.gpsimd.affine_select(out=tri[:, :], in_=tri[:, :], compare_op=ALU.is_gt, fill=0.0, base=0,
                                    pattern=[[1, P]], channel_multiplier=-1).then_inc(S["const"], 1)
            nc.gpsimd.affine_select(out=ident[:, :], in_=ident[:, :], compare_op=ALU.not_equal, fill=1.0, base=0,
                                    pattern=[[-1, P]], channel_multiplier=1).then_inc(S["const"], 1)
            nc.gpsimd.memset(hT_all[:, :, :], 0.0).then_inc(S["root_out"], KD * NT)
            for l in range(LAYERS):
                for c in range(4):
                    pool.wait_ge(s_yst[c], 16 * NT * (l + 1))
                yd = y_dram[l % 2]

                def gather(i, halves=HALVES):
                    for h, half in enumerate(halves):
                        wait(pool, "ix_ready", TURNS * l + 2 * i + h + 1)
                        pool.nop(nofuse=True)
                        for j in half:
                            nc.gpsimd.indirect_dma_start(
                                out=gath[:, j, :], out_offset=None, in_=yd,
                                in_offset=bass.IndirectOffsetOnAxis(ap=idx_ring[:, j:j + 1], axis=0)).then_inc(s_gath[j], 16)

                steps(pool, STEPS - 1, gather)
                gather(STEPS - 1, (range(LAST_TILES),))
            pool.wait_ge(S["zero_st"], 16 * (NT + 2))
            pool.wait_ge(S["slots_made"], 1)
            for t in range(NT):
                for c in range(TOPK):
                    nc.gpsimd.indirect_dma_start(out=xs_dram, out_offset=bass.IndirectOffsetOnAxis(ap=pos[:, c, t:t + 1], axis=0),
                                                 in_=expert_rows(t), in_offset=None).then_inc(S["scat_st"], 16)
            for c in range(2):
                pool.wait_ge(s_ys[c], 16 * (SLOT_T // 2))
            for g in range(NG):
                for c in range(TOPK):
                    b = (2 * g + c) % 4
                    if g >= 2:
                        pool.wait_ge(S["combined"], TOPK * TG * (g - 1))
                    for j in range(TG):
                        nc.gpsimd.indirect_dma_start(out=back[b][:, j, :], out_offset=None, in_=ys_dram,
                                                     in_offset=bass.IndirectOffsetOnAxis(ap=pos[:, c, g * TG + j:g * TG + j + 1], axis=0)).then_inc(s_back[b], 16)

        @block.scalar
        def _(act):
            for b, (o, n0, n1) in enumerate(((idx_i, 0, 4), (idx_i, 4, EC), (dloc, 0, 4), (dloc, 4, EC), (dabs, 0, 4), (dabs, 4, EC))):
                act.wait_ge(S["edge_turned"], b + 1)
                nc.scalar.copy(o[:, n0 * P:n1 * P], bank[b][:, 0:(n1 - n0) * P]).then_inc(S["edge_back"], 1)
            act.wait_ge(S["var_made"], 1)
            nc.scalar.activation(rstd[:, :], mv[:, :, 1], ACT.Sqrt).then_inc(S["sd_made"], 1)
            act.wait_ge(S["gb_in"], 16 * LAYERS)
            def ring(l, i, h):
                half = HALVES[h]
                first = isinstance(i, int) and i == 0
                wait(act, "tile_mm", ETILES * l if first else ETILES * l + STEP * i + half[-1] + 1 - STEP)
                nc.scalar.copy(idx_ring[:, half[0]:half[-1] + 1],
                               idx_i[:, bass.ds(STEP * i + half[0], len(half))]).then_inc(S["ix_ready"], 1)

            def y_even(l, t, c):
                wait(act, "y_mm", 4 * NT * l + 4 * t + c + 1)
                wait(act, s_yst[c], 16 * (NT * l + t))
                nc.scalar.copy(ybuf[:, c, :], bank[c][:, :]).then_inc(S["y_act"], 1)

            def root_back(l, t):
                wait_apart(act, "node_mm", NT * (l - 1) + t + 1)
                for e in range(KD):
                    nc.scalar.activation(hT_all[:, bass.ds(t * P, P), e], bank[4][:, e * P:(e + 1) * P],
                                         ACT.Identity, bias=bias_g[:, l, e:e + 1]).then_inc(S["root_out"], 1)

            def relu(l, t):
                act.wait_ge(S["node_ready"], NT * (l - 1) + t + 1)
                wait_apart(act, "node_mm", NT * (l - 1) + t)
                nc.scalar.activation(stage[:, 0, :, :], features(t), ACT.Relu).then_inc(S["stage_full"], 1)

            def node_whole(l, t):
                relu(l, t)
                y_even(l, t, 0)
                y_even(l, t, 2)
                root_back(l, t)

            def x_stage(i, j):
                wait(act, "xn_turned", TG * i + j + 1)
                wait(act, "y_mm", 4 * (TG * i + j + 1 - TG))
                nc.scalar.copy(stage[:, j, :, :], bank[6 + j % 2][:, 0:D].rearrange("p (k n) -> p k n", k=KD)).then_inc(S["stage_full"], 1)

            def first_y(i, j):
                y_even(0, TG * i + j, 0)
                y_even(0, TG * i + j, 2)

            groups(act, x_stage, first_y)

            def late_stage(t):
                wait(act, "late_turned", t + 1)
                wait(act, "late_mm", t)
                nc.scalar.copy(stage[:, 1, :, :], bank[7][:, 0:D].rearrange("p (k n) -> p k n", k=KD)).then_inc(S["late_staged"], 1)

            def mix_exp():
                act.wait_ge(S["kmax_made"], 1)
                nc.scalar.activation(kT[:, 0:N_NODES], kT[:, 0:N_NODES], ACT.Exp, bias=nkmax, accum_out=ksum).then_inc(S["kexp_made"], 1)

            def sigmoid(t):
                act.wait_ge(S["node_ready"], NT * (LAYERS - 1) + t + 1)
                wait_apart(act, "sg_turned", t)
                nc.scalar.activation(sgT, features(t), ACT.Sigmoid).then_inc(S["sg_made"], 1)

            def deviation(t, n):
                act.wait_ge(S["x2_var"], 2 * t + n + 1)
                r, m = (rstd, mv) if n == 0 else (rstd2, mv2)
                nc.scalar.activation(r[:, 0:1], m[:, 0, 1:2], ACT.Sqrt).then_inc(S["x2_sd"], 1)

            def y_back(t):
                wait(act, "y_turned", t + 1)
                wait(act, "router_mm", t)
                nc.scalar.copy(turned_y, bank[2][:, 0:D].rearrange("p (k n) -> p k n", k=KD)).then_inc(S["y_out"], 1)

            def final_node(t):
                sigmoid(t)
                deviation(t, 0)
                deviation(t, 1)
                y_back(t)

            def rings(l):
                def both(i):
                    for h in range(2):
                        ring(l, i, h)

                steps(act, STEPS - 1, both)
                ring(l, STEPS - 1, 0)

            for l in range(LAYERS):
                outside = act.value_load(flag[0:1, 0:1], min_val=0, max_val=1)
                final = l == LAYERS - 1
                with act.If(outside < 1):
                    def span(m, nodes):
                        ring(l, 2 * m, 0)
                        ring(l, 2 * m, 1)
                        if is_step(l, m, 1, 0):
                            mix_exp()
                        for u in range(ETILES - SPAN * m if is_last(m) else SPAN):
                            if u == HALVES[0][-1]:
                                ring(l, 2 * m + 1, 0)
                            if u == HALVES[1][-1] and not is_last(m):
                                ring(l, 2 * m + 1, 1)
                            for t in beside(l, m, u, "stage"):
                                late_stage(t)
                            for t, at in nodes:
                                if final:
                                    if at.get(u + 2) == 0:
                                        sigmoid(t)
                                    if at.get(u) in (1, 2):
                                        deviation(t, at[u] - 1)
                                    if at.get(u) == 3:
                                        y_back(t)
                                else:
                                    if at.get(u + 2) == 0:
                                        relu(l + 1, t)
                                    if at.get(u) in (0, 2):
                                        y_even(l + 1, t, at[u])
                                    if at.get(u) == 4:
                                        root_back(l + 1, t)

                    edge_loop(span, act)
                with act.Else():
                    if l == 1:
                        mix_exp()
                    rings(l)
                    if l == 0:
                        steps(act, NT, late_stage)
                    if final:
                        steps(act, INNER_T, final_node)
                    else:
                        steps(act, INNER_T, lambda t: node_whole(l + 1, t))
                for t in range(INNER_T, NT):
                    if final:
                        final_node(t)
                    else:
                        node_whole(l + 1, t)

            act.wait_ge(S["router_in"], 1)
            nc.scalar.activation(pr, lg, ACT.Exp).then_inc(S["router_exp"], 1)
            act.wait_ge(S["b1_mm"], 2)
            for e in range(EXP):
                nc.scalar.activation(w1a[:, 1, e * HF:(e + 1) * HF], w1a[:, 1, e * HF:(e + 1) * HF], ACT.Copy,
                                     scale=gcols[:, e, 1:2]).then_inc(S["w_scaled"], 1)

            def rows_back(n, c):
                act.wait_ge(S["xs_turned"], n + 1)
                nc.scalar.copy(xsT[c], bank[0][:, 0:D].rearrange("p (k n) -> p k n", k=KD)).then_inc(S["xs_back"], 1)

            rows_back(0, 0)
            rows_back(1, 1)

            def gelu(s):
                for h in range(2):
                    act.wait_ge(S["hid_pre"], 2 * s + h + 1)
                    nc.scalar.activation(hrow[:, h * 512:(h + 1) * 512], hrow[:, h * 512:(h + 1) * 512], ACT.Gelu).then_inc(S["hid_act"], 1)

            def slot(i):
                for c in range(2):
                    s = 2 * i + c
                    act.wait_ge(S["hid_turned"], 2 * s + 2)
                    nc.scalar.copy(hTq[:, HC // 2:HC, :], bank[4][:, :].rearrange("p (q n) -> p q n", q=HC // 2)).then_inc(S["hid_back_s"], 1)
                    rows_back(s + 2, c)
                    gelu(s + 1)

            gelu(0)
            slot(0)
            with act.Fori(1, SLOT_T // 2) as i:
                slot(i)

        @block.vector
        def _(dve):
            chain = [0]

            def link(ins):
                chain[0] += 1
                ins.then_inc(S["chain_v"], 1)
                dve.wait_ge(S["chain_v"], chain[0])

            dve.wait_ge(S["const"], 9)
            link(nc.vector.tensor_scalar(node_in[:, :], pad_pos[:, 0, :], float(N_NODES), None, ALU.is_lt))
            link(nc.vector.tensor_scalar(rstd2[:, :], node_in[:, :], -1.0, 1.0, ALU.mult, ALU.add))
            link(nc.vector.tensor_scalar(pad_pos[:, 1, :], pad_pos[:, 0, :], float(SLOTS + P - (NT - 1) * P), None, ALU.add))
            link(nc.vector.tensor_scalar(pad_pos[:, 0, :], pad_pos[:, 0, :], float(SLOTS - (NT - 1) * P), None, ALU.add))
            link(nc.vector.tensor_tensor(pad_pos[:, :, :], pad_pos[:, :, :], rstd2[:, :].unsqueeze(1).to_broadcast([P, TOPK, NT]), ALU.mult))
            dve.wait_ge(S["edge_in"], 9 * 16)
            link(nc.vector.tensor_copy(e_dstf, e_dst))
            nc.vector.scalar_tensor_tensor(out=e_idx, in0=e_src, scalar=float(REL), in1=e_typ, op0=ALU.mult, op1=ALU.add)
            link(nc.vector.tensor_reduce(out=e_win, in_=e_dstf, op=ALU.min, axis=AXX))
            link(nc.vector.tensor_scalar(e_win, e_win, float(NP - WIN), None, ALU.min))
            nc.vector.tensor_copy(e_wini, e_win).then_inc(S["edges_made"], 1)
            link(nc.vector.tensor_tensor(e_loc, e_dstf, e_win.unsqueeze(2).to_broadcast([P, EC, P]), ALU.subtract))
            nc.vector.memset(zcol[:, :], 0.0).then_inc(S["edges_made"], 1)
            link(nc.vector.tensor_scalar(e_in, e_dstf, NO_NODE / 2, None, ALU.is_lt))
            link(nc.vector.scalar_tensor_tensor(out=e_in, in0=e_loc, scalar=float(WIN), in1=e_in, op0=ALU.is_ge, op1=ALU.mult))
            link(nc.vector.tensor_reduce(out=e_viol[:, 0:1], in_=e_in.rearrange("p c n -> p (c n)"), op=ALU.add, axis=AXX))
            link(nc.vector.tensor_scalar(e_caught, e_span, float(CATCH_UP * SPAN), None, ALU.is_ge))
            link(nc.vector.tensor_scalar(e_late, e_span, float(BEFORE_LAST * SPAN + STEP), None, ALU.is_ge))
            link(nc.vector.tensor_tensor(e_caught, e_caught, e_late, ALU.add))
            link(nc.vector.tensor_scalar(e_final, e_span, float((SPANS - 1) * SPAN + LAST_READY), None, ALU.is_ge))
            link(nc.vector.tensor_scalar(e_late, e_span, float(SPAN_INV), None, ALU.mult))
            link(nc.vector.tensor_copy(e_span, e_late))
            link(nc.vector.tensor_scalar(e_span, e_span, 16, None, ALU.arith_shift_right))
            link(nc.vector.tensor_tensor(e_late, e_span, e_caught, ALU.add))
            link(nc.vector.tensor_scalar(e_late, e_late, float(SPANS), None, ALU.min))
            link(nc.vector.tensor_tensor(e_late, e_late, e_final, ALU.add))
            link(nc.vector.tensor_scalar(e_late, e_late, float(P), float(-P), ALU.mult, ALU.add))
            link(nc.vector.tensor_scalar(e_late, e_late, float(NP - WIN), None, ALU.min))
            link(nc.vector.tensor_tensor(e_late, e_win, e_late, ALU.is_lt))
            link(nc.vector.tensor_reduce(out=e_viol[:, 1:2], in_=e_late, op=ALU.add, axis=AXX))
            nc.vector.tensor_tensor(e_viol[:, 0:1], e_viol[:, 0:1], e_viol[:, 1:2], ALU.add).then_inc(S["edges_made"], 1)
            for g in range(NG):
                dve.wait_ge(s_x[g], 16 if g < NG - 1 else 32)
                for t in range(TG * g, TG * (g + 1)):
                    last = nc.vector.bn_stats(stats[:, t, :], xtok[:, t, :])
            link(last)
            for t in range(NT):
                last = nc.vector.bn_aggr(mv[:, t, :], stats[:, t, :])
            link(last)
            nc.vector.tensor_scalar(mv[:, :, 1], mv[:, :, 1], EPS, None, ALU.add).then_inc(S["var_made"], 1)
            dve.wait_ge(S["viol_sum"], 1)
            nc.vector.tensor_scalar(flag[:, :], bank[6][:, 0:1], 1.0, None, ALU.min).then_inc(S["flag_set"], 1)
            dve.wait_ge(S["sd_made"], 1)
            link(nc.vector.reciprocal(rstd[:, :], rstd[:, :]))

            def y_odd(l, t, c):
                wait(dve, "y_mm", 4 * NT * l + 4 * t + c + 1)
                wait(dve, s_yst[c], 16 * (NT * l + t))
                nc.vector.tensor_copy(ybuf[:, c, :], bank[c][:, :]).then_inc(S["y_dve"], 1)

            def x_normed(i, j):
                t = TG * i + j
                wait(dve, "xn_turned", t + 1 - TG)
                nc.vector.tensor_scalar(xnt[:, j, :], tile_of(xtok, t), mv[:, bass.ds(t, 1), 0],
                                        rstd[:, bass.ds(t, 1)], ALU.subtract, ALU.mult).then_inc(S["xn_made"], 1)

            def first_y(i, j):
                y_odd(0, TG * i + j, 1)
                y_odd(0, TG * i + j, 3)

            groups(dve, x_normed, first_y, ahead_first=True)
            dve.wait_ge(S["mixw_in"], 48)
            dve.wait_ge(S["xn_turned"], NT)

            def late_rows(t):
                wait(dve, "late_turned", t)
                nc.vector.tensor_scalar(xnt[:, 0, :], tile_of(xtok, t), mv[:, bass.ds(t, 1), 0],
                                        rstd[:, bass.ds(t, 1)], ALU.subtract, ALU.mult).then_inc(S["late_made"], 1)
                wait(dve, "late_made", t + 1)
                nc.vector.tensor_tensor(tile_of(xtok, t), tile_of(xtok, t), bout_sb, ALU.add).then_inc(S["x_biased"], 1)

            def late_qkv(t):
                wait(dve, "qkv_mm", t + 1)
                nc.vector.tensor_copy(qT[:, bass.ds(t * P, P)], bank[7][:, 0:P])
                nc.vector.tensor_copy(kT[:, bass.ds(t * P, P)], bank[7][:, P:2 * P])
                nc.vector.tensor_copy(tile_of(vtok, t), bank[7][:, 2 * P:3 * P]).then_inc(S["qkv_out"], 1)

            def late_add(t, n):
                wait(dve, "tile_add", n)
                wait(dve, "late_mm", t + 1)
                for e in range(KD):
                    a = hT_all[:, bass.ds(t * P, P), e]
                    nc.vector.scalar_tensor_tensor(out=a, in0=bank[7][:, e * P:(e + 1) * P], scalar=bias_g[:, 0, e:e + 1], in1=a,
                                                   op0=ALU.add, op1=ALU.add).then_inc(S["late_added"], 1)
                wait(dve, "late_added", KD * (t + 1))

            def late_whole(t):
                late_rows(t)
                late_qkv(t)
                late_add(t, 0)

            def mix_max():
                dve.wait_ge(S["qkv_out"], NT)
                link(nc.vector.reduce_max(nkmax, kT[:, 0:N_NODES], AXX))
                nc.vector.tensor_scalar(nkmax, nkmax, -1.0, None, ALU.mult).then_inc(S["kmax_made"], 1)

            def mix_key(t):
                dve.wait_ge(S["k_turned"], t + 1)
                nc.vector.tensor_copy(ktok[:, t % 2, :], bank[t % 2][:, 0:P]).then_inc(S["k_out"], 1)

            def mix_context():
                link(nc.vector.reciprocal(krec, ksum))
                link(nc.vector.tensor_scalar(krec, krec, float(DH) ** -0.5, None, ALU.mult))
                link(nc.vector.memset(ctxT, 0.0))
                dve.wait_ge(S["ctx_mm"], NT)
                for h in range(HEADS):
                    r = slice(h * DH, (h + 1) * DH)
                    last = nc.vector.tensor_copy(ctxT[r, r], bank[2][r, r])
                last.then_inc(S["ctx_out"], 1)
                dve.wait_ge(S["mctx_mm"], 1)
                nc.vector.tensor_scalar(mctx, bank[3][:, 0:D], krec, None, ALU.mult).then_inc(S["mctx_out"], 1)

            def mix_node(t):
                dve.wait_ge(S["mix_mm"], t + 1)
                nc.vector.tensor_tensor(xtok[:, t, :], xtok[:, t, :], bank[t % 2][:, 0:D], ALU.add).then_inc(S["mix_add"], 1)

            dve.wait_ge(S["win_in"], 16)
            dve.wait_ge(S["edge_back"], 6)

            def norm_step(t, n, ins):
                ins.then_inc(S["norm_step"], 1)
                wait_apart(dve, "norm_step", 6 * t + n)

            def x2_node(t):
                wait(dve, "xn2_made", t)
                wait(dve, "sg_turned", t + 1)
                nc.vector.tensor_tensor(tile_of(xtok, t), tile_of(xtok, t), bank[1][:, 0:D], ALU.add).then_inc(S["sg_add"], 1)
                wait_apart(dve, "sg_add", t + 1)
                norm_step(t, 1, nc.vector.bn_stats(stats[:, 0, :], tile_of(xtok, t)))
                norm_step(t, 2, nc.vector.bn_aggr(mv[:, 0, :], stats[:, 0, :]))
                nc.vector.tensor_scalar(mv[:, 0, 1:2], mv[:, 0, 1:2], EPS, None, ALU.add).then_inc(S["x2_var"], 1)

            def y_node(t):
                wait(dve, "x2_sd", 2 * t + 1)
                norm_step(t, 3, nc.vector.reciprocal(rstd[:, 0:1], rstd[:, 0:1]))
                wait(dve, "y_turned", t)
                nc.vector.tensor_scalar(yrow, tile_of(xtok, t), mv[:, 0, 0:1], rstd[:, 0:1],
                                        ALU.subtract, ALU.mult).then_inc(S["y_made"], 1)
                wait(dve, "y_made", t + 1)
                norm_step(t, 4, nc.vector.bn_stats(stats[:, 1, :], yrow))
                norm_step(t, 5, nc.vector.bn_aggr(mv2[:, 0, :], stats[:, 1, :]))
                nc.vector.tensor_scalar(mv2[:, 0, 1:2], mv2[:, 0, 1:2], EPS, None, ALU.add).then_inc(S["x2_var"], 1)

            def xn2_node(t):
                wait(dve, "x2_sd", 2 * t + 2)
                norm_step(t, 6, nc.vector.reciprocal(rstd2[:, 0:1], rstd2[:, 0:1]))
                nc.vector.tensor_scalar(expert_rows(t), yrow, mv2[:, 0, 0:1],
                                        rstd2[:, 0:1], ALU.subtract, ALU.mult).then_inc(S["xn2_made"], 1)

            def final_node(t):
                x2_node(t)
                y_node(t)
                xn2_node(t)

            for l in range(LAYERS):
                final = l == LAYERS - 1
                if final:
                    dve.wait_ge(S["ffw_in"], 16 * FFW)
                    link(nc.vector.memset(bsel, 0.0))
                    for e in range(EXP):
                        last = nc.vector.tensor_copy(bsel[:, e, :, e], bcols[:, :, e])
                    last.then_inc(S["bsel_made"], 1)
                dve.wait_ge(S["root_out"], KD * NT * (l + 1))
                outside = dve.value_load(flag[0:1, 0:1], min_val=0, max_val=1)
                links = chain[0]
                with dve.If(outside < 1):
                    def hot(i, half):
                        nc.vector.tensor_tensor(
                            onehot[:, half[0]:half[-1] + 1, :],
                            iota_w[:, 0:WIN].unsqueeze(1).to_broadcast([P, len(half), WIN]),
                            dloc[:, bass.ds(STEP * i + half[0], len(half))].unsqueeze(2).to_broadcast([P, len(half), WIN]),
                            ALU.is_equal).then_inc(S["hot_ready"], 1)

                    def span(m, nodes):
                        for a in range(2):
                            i = 2 * m + a
                            tiles = LAST_TILES if a and is_last(m) else STEP
                            _, wins = nc.values_load_multi_w_load_instructions(
                                win_row[0:1, bass.ds(STEP * i, tiles)], engines=(dve.engine,), min_val=0, max_val=NP - WIN,
                                skip_runtime_bounds_check_because="clamped when they were made")
                            for h, half in enumerate(HALVES):
                                for j in half[:tiles - half[0]] if tiles > half[0] else ():
                                    u = a * STEP + j
                                    n = ETILES * l + SPAN * m + u
                                    for t, at in nodes:
                                        if u == ready_at(at):
                                            dve.wait_ge(S["tile_add"], n)
                                            nc.vector.memset(zcol[:, :], 0.0).then_inc(S["node_ready"], 1)
                                    wait(dve, "tile_mm", n + 1)
                                    wait(dve, "tile_add", n)
                                    acc = hT_all[:, bass.ds(wins[j], WIN), :]
                                    nc.vector.tensor_tensor(acc, acc, bank[5 + u % 2][:, 0:KD * WIN].rearrange("p (k n) -> p n k", k=KD),
                                                            ALU.add).then_inc(S["tile_add"], 1)
                                    for t, at in nodes:
                                        if final and at.get(u) == 1:
                                            x2_node(t)
                                        if final and at.get(u) == 2:
                                            y_node(t)
                                        if final and at.get(u) == 4:
                                            xn2_node(t)
                                        if not final and at.get(u) in (1, 3):
                                            y_odd(l + 1, t, at[u])
                                    for t in beside(l, m, u, "rows"):
                                        late_rows(t)
                                    for t in beside(l, m, u, "qkv_out"):
                                        late_qkv(t)
                                    for t in beside(l, m, u, "add"):
                                        late_add(t, n + 1)
                                    if is_step(l, m, 1, 0) and 0 <= u - MIX_AT < NT:
                                        mix_key(u - MIX_AT)
                                    if mix_tile(l, m, u) is not None:
                                        mix_node(mix_tile(l, m, u))
                                if not (is_last(m) and a + h):
                                    hot(i + 1, half)

                        if is_step(l, m, 1, 0):
                            mix_context()

                    for half in HALVES:
                        hot(0, half)
                    if l == 1:
                        dve.wait_ge(S["x_biased"], NT)
                        mix_max()
                    edge_loop(span, dve)
                    dve.wait_ge(S["tile_add"], ETILES * (l + 1))
                with dve.Else():
                    chain[0] = links
                    if l == 1:
                        dve.wait_ge(S["x_biased"], NT)
                        mix_max()
                        for t in range(NT):
                            mix_key(t)
                        mix_context()
                        for t in range(NT):
                            mix_node(t)
                    with dve.Fori(0, ETILES) as n:
                        nc.vector.tensor_copy(gcol[:, 0:1], dabs[:, bass.ds(n, 1)]).then_inc(S["gen_hot"], 1)
                        with dve.Fori(0, NGW) as v:
                            g = (n + ETILES * l) * NGW + v
                            dve.wait_ge(S["gen_hot"], (n + ETILES * l) * (2 * NGW + 1) + v * 2 + 1)
                            nc.vector.tensor_scalar(ghot, iota_w[:, :], gcol[:, 0:1], None, ALU.is_equal).then_inc(S["gen_hot"], 1)
                            dve.wait_ge(S["gen_hot"], (n + ETILES * l) * (2 * NGW + 1) + v * 2 + 2)
                            nc.vector.tensor_scalar(gcol[:, 0:1], gcol[:, 0:1], float(-GWIN), None, ALU.add).then_inc(S["gen_hot"], 1)
                            dve.wait_ge(S["gen_mm"], g + 1)
                            for k in range(KD):
                                a = hT_all[:, bass.ds(v * GWIN, GWIN), k]
                                nc.vector.tensor_tensor(a, a, bank[5 + k][:, 0:GWIN], ALU.add).then_inc(S["gen_add"], 1)
                            dve.wait_ge(S["gen_add"], (g + 1) * KD)
                    if l == 0:
                        steps(dve, NT, late_whole)
                    nc.vector.memset(zcol[:, :], 0.0).then_inc(S["node_ready"], INNER_T)
                    if final:
                        steps(dve, INNER_T, final_node)
                    else:
                        with dve.Fori(0, INNER_T) as t:
                            y_odd(l + 1, t, 1)
                            y_odd(l + 1, t, 3)
                nc.vector.memset(zcol[:, :], 0.0).then_inc(S["layer_done"], 1)
                dve.wait_ge(S["layer_done"], l + 1)
                nc.vector.memset(zcol[:, :], 0.0).then_inc(S["node_ready"], NT - INNER_T)
                for t in range(INNER_T, NT):
                    if final:
                        final_node(t)
                    else:
                        y_odd(l + 1, t, 1)
                        y_odd(l + 1, t, 3)

            bc = lambda a: a.unsqueeze(2).to_broadcast([P, NT, EXP])
            dve.wait_ge(S["router_mm"], NT)
            link(nc.vector.tensor_copy(lg, bank[3][:, 0:NT * EXP].rearrange("p (t e) -> p t e", t=NT)))
            link(nc.vector.tensor_reduce(out=rmax, in_=lg, op=ALU.max, axis=AXX))
            nc.vector.tensor_tensor(lg, lg, bc(rmax), ALU.subtract).then_inc(S["router_in"], 1)
            dve.wait_ge(S["router_exp"], 1)
            link(nc.vector.tensor_reduce(out=rsum, in_=pr, op=ALU.add, axis=AXX))
            link(nc.vector.reciprocal(rrec, rsum))
            link(nc.vector.tensor_tensor(pr, pr, bc(rrec), ALU.mult))
            for t in range(NT):
                last = nc.vector.max(top[:, t, :], pr[:, t, :])
            link(last)
            for t in range(NT):
                last = nc.vector.max_index(topi[:, t, :], top[:, t, :], pr[:, t, :])
            link(last)
            link(nc.vector.tensor_copy(topf, topi))
            link(nc.vector.tensor_tensor(rsum, top[:, :, 0], top[:, :, 1], ALU.add))
            link(nc.vector.reciprocal(rrec, rsum))
            link(nc.vector.tensor_tensor(top[:, :, 0:2], top[:, :, 0:2], rrec.unsqueeze(2).to_broadcast([P, NT, 2]), ALU.mult))
            eid = iota_w[:, 0:EXP].unsqueeze(1).to_broadcast([P, NT, EXP])
            real = bc(node_in[:, :])
            for c in range(TOPK):
                link(nc.vector.tensor_tensor(hit[c], eid, bc(topf[:, :, c]), ALU.is_equal))
            link(nc.vector.tensor_tensor(chosen, hit[0], hit[1], ALU.add))
            nc.vector.tensor_tensor(chosen, chosen, real, ALU.mult).then_inc(S["sel_made"], 1)
            dve.wait_ge(S["sel_mm"], 2)
            link(nc.vector.tensor_copy(before, bank[5][:, 0:NT * EXP].rearrange("p (t e) -> p t e", t=NT)))
            link(nc.vector.tensor_copy(tile_cnt, bank[6][:, 0:NT * EXP].rearrange("p (t e) -> p e t", t=NT)))
            for e in range(EXP):
                last = nc.vector.tensor_tensor_scan(upto[:, e, :], ones[:, 0:NT], tile_cnt[:, e, :], 0.0, ALU.mult, ALU.add)
            link(last)
            link(nc.vector.tensor_scalar(cnt_i, upto[:, :, NT - 1], float(P - 1), None, ALU.add))
            link(nc.vector.tensor_scalar(cnt_i, cnt_i, 7, None, ALU.arith_shift_right))
            link(nc.vector.tensor_copy(ntl, cnt_i))
            link(nc.vector.tensor_tensor_scan(tend, ones[:, 0:EXP], ntl, 0.0, ALU.mult, ALU.add))
            link(nc.vector.tensor_tensor(sbase, tend, ntl, ALU.subtract))
            link(nc.vector.tensor_scalar(sbase, sbase, float(P), None, ALU.mult))
            link(nc.vector.tensor_tensor(upto, upto, tile_cnt, ALU.subtract))
            link(nc.vector.tensor_tensor(upto, upto, sbase.unsqueeze(2).to_broadcast([P, EXP, NT]), ALU.add))
            link(nc.vector.tensor_tensor(before, before, upto.rearrange("p e t -> p t e"), ALU.add))
            for c in range(TOPK):
                link(nc.vector.tensor_tensor(lg, hit[c], before, ALU.mult))
                link(nc.vector.tensor_reduce(out=spos, in_=lg, op=ALU.add, axis=AXX))
                link(nc.vector.tensor_tensor(spos, spos, node_in[:, :], ALU.mult))
                ins = nc.vector.tensor_tensor(pos[:, c, :], spos, pad_pos[:, c, :], ALU.add)
                link(ins) if c == 0 else ins.then_inc(S["slots_made"], 1)
            link(nc.vector.tensor_tensor(past, iota_w[:, 0:XS_T].unsqueeze(2).to_broadcast([P, XS_T, EXP]),
                                         tend.unsqueeze(1).to_broadcast([P, XS_T, EXP]), ALU.is_ge))
            link(nc.vector.tensor_reduce(out=slot_expf, in_=past, op=ALU.add, axis=AXX))
            nc.vector.tensor_scalar(slot_exp, slot_expf, float(EXP - 1), None, ALU.min).then_inc(S["slots_made"], 1)
            for h in range(2):
                dve.wait_ge(S["b1_mm"], h + 1)
                o = b1_sb[0:EXP, h * 512:(h + 1) * 512]
                nc.vector.tensor_tensor(o, o, bank[4 if h == 0 else 7][0:EXP, :], ALU.add).then_inc(S["b1_added"], 1)
            for e in range(EXP):
                nc.vector.tensor_scalar(w1a[:, 0, e * HF:(e + 1) * HF], w1a[:, 0, e * HF:(e + 1) * HF], gcols[:, e, 0:1], None,
                                        ALU.mult).then_inc(S["w_scaled"], 1)

            def hidden_in(s, c, n_bias):
                dve.wait_ge(s_bias[c], n_bias)
                wait(dve, "hid_turned", 2 * s)
                for h in range(2):
                    dve.wait_ge(S["hid_mm"], 2 * s + h + 1)
                    nc.vector.tensor_tensor(hrow[:, h * 512:(h + 1) * 512], bank[1 + h][:, :], b1t[c][:, h * 512:(h + 1) * 512],
                                            ALU.add).then_inc(S["hid_pre"], 1)

            def slot(i):
                for c in range(2):
                    s = 2 * i + c
                    dve.wait_ge(S["hid_turned"], 2 * s + 1)
                    nc.vector.tensor_copy(hTq[:, 0:HC // 2, :], bank[3][:, :].rearrange("p (q n) -> p q n", q=HC // 2)).then_inc(S["hid_back_v"], 1)
                    hidden_in(s + 1, 1 - c, (i + c) * 32 + 32)
                    dve.wait_ge(S["out_mm"], s + 1)
                    wait(dve, s_ys[c], i * 16)
                    nc.vector.tensor_tensor(orow[c], bank[5 + c][:, 0:D], b2t[c], ALU.add).then_inc(S["out_back"], 1)

            dve.wait_ge(S["scat_st"], 16 * TOPK * NT)
            hidden_in(0, 0, 32)
            slot(0)
            with dve.Fori(1, SLOT_T // 2) as i:
                slot(i)
            for g in range(NG):
                for c in range(TOPK):
                    b = (2 * g + c) % 4
                    dve.wait_ge(s_back[b], 16 * TG * ((2 * g + c) // 4 + 1))
                    if c:
                        dve.wait_ge(S["combined"], TG * (2 * g + 1))
                    for j in range(TG):
                        t = g * TG + j
                        nc.vector.scalar_tensor_tensor(out=xtok[:, t, :], in0=back[b][:, j, :], scalar=top[:, t, c:c + 1],
                                                       in1=xtok[:, t, :], op0=ALU.mult, op1=ALU.add).then_inc(S["combined"], 1)

        @block.tensor
        def _(pe):
            pe.wait_ge(S["const"], 9)
            pe.wait_ge(S["edges_made"], 2)
            for b, (a, n0, n1) in enumerate(((e_idx, 0, 4), (e_idx, 4, EC), (e_loc, 0, 4), (e_loc, 4, EC), (e_dstf, 0, 4), (e_dstf, 4, EC))):
                for c in range(n0, n1):
                    m = nc.tensor.transpose(bank[b][:, (c - n0) * P:(c - n0 + 1) * P], a[:, c, :], ident[:, :])
                m.then_inc(S["edge_turned"], 1)
            pe.wait_ge(S["edges_made"], 3)
            nc.tensor.matmul(bank[6][:, 0:1], ones[:, :], e_viol[:, 0:1], start=True, stop=True).then_inc(S["viol_sum"], 1)
            pe.wait_ge(S["edge_back"], 6)
            pe.wait_ge(S["flag_set"], 1)

            def y_piece(l, t, j, c):
                wait(pe, "y_act" if c % 2 == 0 else "y_dve", 2 * NT * l + 2 * t + c // 2 - 1)
                for k in range(KD):
                    m = nc.tensor.matmul(bank[c][:, :], stage[:, j, k, :], wrel[:, k, c * 512:(c + 1) * 512],
                                         start=k == 0, stop=k == KD - 1)
                m.then_inc(S["y_mm"], 1)

            def root_piece(l, t, j):
                wait(pe, "root_out", KD * (NT * l + t))
                for e in range(KD):
                    for k in range(KD):
                        m = nc.tensor.matmul(bank[4][:, e * P:(e + 1) * P], wroot[:, k, e * P:(e + 1) * P], stage[:, j, k, :],
                                             start=k == 0, stop=k == KD - 1)
                m.then_inc(S["node_mm"], 1)

            def node_piece(l, t, p):
                if p == 0:
                    pe.wait_ge(S["stage_full"], NT * l + t + 1)
                if p < 4:
                    y_piece(l, t, 0, p)
                else:
                    root_piece(l, t, 0)

            pe.wait_ge(S["wrel_in"], 48)
            pe.wait_ge(S["mixw_in"], 48)
            pe.wait_ge(S["win_out"], 16)

            def x_turn(i, j):
                t = TG * i + j
                wait(pe, "xn_made", t + 1)
                wait(pe, "stage_full", t if j == 0 else t - 1)
                for k in range(KD):
                    m = nc.tensor.transpose(bank[6 + j % 2][:, k * P:(k + 1) * P], xnt[:, j, k * P:(k + 1) * P], ident[:, :])
                m.then_inc(S["xn_turned"], 1)

            def first_y(i, j):
                wait(pe, "stage_full", TG * i + j + 1)
                for c in range(4):
                    y_piece(0, TG * i + j, j, c)

            groups(pe, x_turn, first_y)

            def late_turn(t):
                wait(pe, "late_made", t + 1)
                wait(pe, "late_added", KD * t)
                for k in range(KD):
                    m = nc.tensor.transpose(bank[7][:, k * P:(k + 1) * P], xnt[:, 0, k * P:(k + 1) * P], ident[:, :])
                m.then_inc(S["late_turned"], 1)

            def late_qkv(t):
                wait(pe, "late_staged", t + 1)
                for o in range(3):
                    for k in range(KD):
                        w = wqkv_sb[:, k, o * P:(o + 1) * P]
                        h = stage[:, 1, k, :]
                        m = nc.tensor.matmul(bank[7][:, o * P:(o + 1) * P], h if o == 2 else w, w if o == 2 else h,
                                             start=k == 0, stop=k == KD - 1)
                m.then_inc(S["qkv_mm"], 1)

            def late_root(t):
                wait(pe, "qkv_out", t + 1)
                for e in range(KD):
                    for k in range(KD):
                        m = nc.tensor.matmul(bank[7][:, e * P:(e + 1) * P], wroot0[:, k, e * P:(e + 1) * P], stage[:, 1, k, :],
                                             start=k == 0, stop=k == KD - 1)
                m.then_inc(S["late_mm"], 1)

            def late_whole(t):
                late_turn(t)
                late_qkv(t)
                late_root(t)

            def mix_key(t):
                if t == 0:
                    pe.wait_ge(S["kexp_made"], 1)
                    pe.wait_ge(S["y_act"], 2 * NT * 2)
                    pe.wait_ge(S["y_dve"], 2 * NT * 2)
                if t < NT:
                    rows = P if t < NT - 1 else LAST
                    if t >= 2:
                        pe.wait_ge(S["k_out"], t - 1)
                    nc.tensor.transpose(bank[t % 2][0:rows, 0:P], kT[:, t * P:t * P + rows], ident[:, :]).then_inc(S["k_turned"], 1)
                if t >= 1:
                    rows = P if t < NT else LAST
                    pe.wait_ge(S["k_out"], t)
                    nc.tensor.matmul(bank[2][:, 0:P], vtok[0:rows, t - 1, :], ktok[0:rows, (t - 1) % 2, :],
                                     start=t == 1, stop=t == NT).then_inc(S["ctx_mm"], 1)

            def mix_context():
                pe.wait_ge(S["ctx_out"], 1)
                nc.tensor.matmul(bank[3][:, 0:D], ctxT, wout_sb, start=True, stop=True).then_inc(S["mctx_mm"], 1)

            def mix_node(t, l=1):
                if t == 0:
                    pe.wait_ge(S["mctx_out"], 1)
                if t in MIX_END:
                    pe.wait_ge(S["y_act"], 2 * NT * (l + 1))
                    pe.wait_ge(S["y_dve"], 2 * NT * (l + 1))
                if t >= 2:
                    pe.wait_ge(S["mix_add"], t - 1)
                nc.tensor.matmul(bank[t % 2][:, 0:D], qT[:, t * P:(t + 1) * P], mctx, start=True, stop=True).then_inc(S["mix_mm"], 1)
                if t + 1 in MIX_END:
                    pe.wait_ge(S["mix_add"], t + 1)

            def final_piece(t, p):
                if p == 0:
                    wait(pe, "sg_made", t + 1)
                    wait(pe, "sg_add", t)
                    for k in range(KD):
                        m = nc.tensor.transpose(bank[1][:, k * P:(k + 1) * P], sgT[:, k, :], ident[:, :])
                    m.then_inc(S["sg_turned"], 1)
                if p == 3:
                    wait(pe, "y_made", t + 1)
                    wait(pe, "y_out", t)
                    for k in range(KD):
                        m = nc.tensor.transpose(bank[2][:, k * P:(k + 1) * P], yrow[:, k * P:(k + 1) * P], ident[:, :])
                    m.then_inc(S["y_turned"], 1)
                if p == 4:
                    wait(pe, "y_out", t + 1)
                    o = bank[3][:, bass.ds(t * EXP, EXP)]
                    for k in range(KD):
                        nc.tensor.matmul(o, turned_y[:, k, :], wr_sb[:, k, :], start=k == 0, stop=False)
                    nc.tensor.matmul(o, ones[0:1, :], br_sb[0:1, :], start=False, stop=True).then_inc(S["router_mm"], 1)

            def fold(h):
                pe.wait_ge(s_wexp[0], 16 * KD * EXP)
                pe.wait_ge(S["bsel_made"], 1)
                for e in range(EXP):
                    for k in range(KD):
                        m = nc.tensor.matmul(bank[4 if h == 0 else 7][0:EXP, :], bsel[:, e, k, :],
                                             w1a[:, k, e * HF + h * 512:e * HF + (h + 1) * 512],
                                             start=e == 0 and k == 0, stop=e == EXP - 1 and k == KD - 1)
                m.then_inc(S["b1_mm"], 1)

            for l in range(LAYERS):
                final = l == LAYERS - 1
                if final:
                    pe.wait_ge(S["ffw_in"], 16 * FFW)
                    pe.wait_ge(S["y_act"], 2 * NT * LAYERS)
                    pe.wait_ge(S["y_dve"], 2 * NT * LAYERS)
                    pe.wait_ge(S["root_out"], KD * NT * LAYERS)
                else:
                    pe.wait_ge(S["wrel_in"], 48 * (l + 2))
                outside = pe.value_load(flag[0:1, 0:1], min_val=0, max_val=1)
                with pe.If(outside < 1):
                    def span(m, nodes):
                        for a in range(2):
                            i = 2 * m + a
                            for j in range(LAST_TILES if a and is_last(m) else STEP):
                                u = a * STEP + j
                                if j in (HALVES[0][0], HALVES[1][0]):
                                    wait(pe, "hot_ready", TURNS * l + 2 * i + (1 if j == 0 else 2))
                                wait(pe, s_gath[j], gathered(l, i, j))
                                wait(pe, "tile_add", ETILES * l + SPAN * m + u - 1)
                                for k in range(KD):
                                    mm = nc.tensor.matmul(bank[5 + u % 2][:, k * WIN:(k + 1) * WIN], gath[:, j, k * P:(k + 1) * P],
                                                          onehot[:, j, :], start=True, stop=True)
                                mm.then_inc(S["tile_mm"], 1)
                                for t, at in nodes:
                                    if u in at:
                                        final_piece(t, at[u]) if final else node_piece(l + 1, t, at[u])
                                for t in beside(l, m, u, "turn"):
                                    late_turn(t)
                                for t in beside(l, m, u, "qkv"):
                                    late_qkv(t)
                                for t in beside(l, m, u, "root"):
                                    late_root(t)
                                if is_step(l, m, 1, 0) and 0 <= u - MIX_AT <= NT:
                                    mix_key(u - MIX_AT)
                                if mix_tile(l, m, u) is not None:
                                    mix_node(mix_tile(l, m, u), l)
                        if is_step(l, m, 1, 0):
                            mix_context()

                    edge_loop(span, pe)
                with pe.Else():
                    if l == 1:
                        for t in range(NT + 1):
                            mix_key(t)
                        mix_context()
                        for t in range(NT):
                            mix_node(t)

                    def windows(i, tiles):
                        for j in range(tiles):
                            n = ETILES * l + i * STEP + j
                            pe.wait_ge(s_gath[j], gathered(l, i, j))
                            pe.nop(nofuse=True)
                            with pe.Fori(0, NGW) as v:
                                pe.wait_ge(S["gen_hot"], n * (2 * NGW + 1) + v * 2 + 2)
                                for k in range(KD):
                                    m = nc.tensor.matmul(bank[5 + k][:, 0:GWIN], gath[:, j, k * P:(k + 1) * P], ghot,
                                                         start=True, stop=True)
                                m.then_inc(S["gen_mm"], 1)
                            pe.wait_ge(S["gen_add"], (n + 1) * NGW * KD)
                            pe.nop(nofuse=True).then_inc(S["tile_mm"], 1)

                    with pe.Fori(0, STEPS - 1) as i:
                        windows(i, STEP)
                    windows(STEPS - 1, LAST_TILES)
                    if l == 0:
                        steps(pe, NT, late_whole)

                    def final_pieces(t):
                        for p in range(5):
                            final_piece(t, p)

                    if final:
                        steps(pe, INNER_T, final_pieces)
                    else:
                        with pe.Fori(0, INNER_T) as t:
                            for p in range(5):
                                node_piece(l + 1, t, p)
                for t in range(INNER_T, NT):
                    for p in range(5):
                        final_piece(t, p) if final else node_piece(l + 1, t, p)

            pe.wait_ge(S["sel_made"], 1)
            flat = chosen.rearrange("p t e -> p (t e)")
            nc.tensor.matmul(bank[5][:, 0:NT * EXP], tri[:, :], flat, start=True, stop=True).then_inc(S["sel_mm"], 1)
            nc.tensor.matmul(bank[6][:, 0:NT * EXP], ones[:, :], flat, start=True, stop=True).then_inc(S["sel_mm"], 1)

            for h in range(2):
                fold(h)

            def turn_rows(s, c):
                wait(pe, "xs_back", s)
                pe.wait_ge(s_xs[c], 16)
                for k in range(KD):
                    m = nc.tensor.transpose(bank[0][:, k * P:(k + 1) * P], xs[c][:, k * P:(k + 1) * P], ident[:, :])
                m.then_inc(S["xs_turned"], 1)

            def hidden(s, c):
                e = pe.value_load(slot_exp[0:1, bass.ds(s, 1)], min_val=0, max_val=EXP - 1)
                pe.wait_ge(S["xs_back"], s + 1)
                for h in range(2):
                    wait(pe, "hid_pre", 2 * s + h - 1)
                    for k in range(KD):
                        m = nc.tensor.matmul(bank[1 + h][:, :], xsT[c][:, k, :], w1a[:, k, bass.ds(e * HF + h * 512, 512)],
                                             start=k == 0, stop=k == KD - 1)
                    m.then_inc(S["hid_mm"], 1)

            def slot(i):
                for c in range(2):
                    s = 2 * i + c
                    for h in range(2):
                        pe.wait_ge(S["hid_act"], 2 * s + h + 1)
                        wait(pe, "hid_back_s" if h else "hid_back_v", s)
                        for q in range(HC // 2):
                            m = nc.tensor.transpose(bank[3 + h][:, q * P:(q + 1) * P], hrow[:, h * 512 + q * P:h * 512 + (q + 1) * P], ident[:, :])
                        m.then_inc(S["hid_turned"], 1)
                    hidden(s + 1, 1 - c)
                    pe.wait_ge(S["xs_back"], s + 2)
                    pe.wait_ge(s_xs[c], i * 16 + 32)
                    for k in range(KD):
                        m = nc.tensor.transpose(bank[0][:, k * P:(k + 1) * P], xs[c][:, k * P:(k + 1) * P], ident[:, :])
                    m.then_inc(S["xs_turned"], 1)
                    e = pe.value_load(slot_exp[0:1, bass.ds(s, 1)], min_val=0, max_val=EXP - 1)
                    pe.wait_ge(S["hid_back_v"], s + 1)
                    pe.wait_ge(S["hid_back_s"], s + 1)
                    wait(pe, "out_back", s - 1)
                    for q in range(HC):
                        m = nc.tensor.matmul(bank[5 + c][:, 0:D], hTq[:, q, :], w2a[:, q, bass.ds(e * D, D)],
                                             start=q == 0, stop=q == HC - 1)
                    m.then_inc(S["out_mm"], 1)

            pe.wait_ge(S["slots_made"], 2)
            pe.wait_ge(S["w_scaled"], 2 * EXP)
            pe.wait_ge(S["b1_added"], 2)
            pe.wait_ge(s_wexp[1], 16 * HC)
            turn_rows(0, 0)
            turn_rows(1, 1)
            hidden(0, 0)
            slot(0)
            with pe.Fori(1, SLOT_T // 2) as i:
                slot(i)


_INS = ["x", "src", "dst", "edge_type_8", "L0_gnn_weights", "L0_gnn_roots", "L0_gnn_biases", "L0_mix_W_qkv",
        "L0_mix_W_out", "L0_mix_b_out", "L0_ffn_Wr", "L0_ffn_br", "L0_ffn_ln_g", "L0_ffn_ln_b",
        "L0_ffn_W1", "L0_ffn_b1", "L0_ffn_W2", "L0_ffn_b2"]


def kernel(**inputs):
    import numpy as _np
    import concourse.bacc as _bacc
    from concourse import mybir as _mybir
    from concourse.bass_utils import run_bass_kernel_spmd as _run

    nc = _bacc.Bacc("TRN2", target_bir_lowering=False, num_devices=1)
    arrays, args = {}, []
    for name in _INS:
        a = _np.ascontiguousarray(inputs[name])
        arrays[f"in_{name}_dram"] = a
        args.append(nc.dram_tensor(f"in_{name}_dram", a.shape, _mybir.dt.from_np(a.dtype), kind="ExternalInput").ap())
    args.append(nc.dram_tensor("out_0_dram", (N_NODES, D), _mybir.dt.float32, kind="ExternalOutput").ap())
    gps_layer(nc, *args)
    r = _run(nc, [arrays], core_ids=[0])
    return r.results[0]["out_0_dram"]
```
